# Optimizing a Trainium2 kernel written in Bass

```python
import numpy as np
import jax
import jax.numpy as jnp

def _softmax(x, axis=-1):
    return jax.nn.softmax(x, axis=axis)

def _gelu(x):
    return jax.nn.gelu(x, approximate=True)

def _silu(x):
    return jax.nn.silu(x)

def _sigmoid(x):
    return jax.nn.sigmoid(x)

def _layernorm(x, axis=-1, eps=1e-05):
    m = jnp.mean(x, axis=axis, keepdims=True)
    v = jnp.var(x, axis=axis, keepdims=True)
    return (x - m) / jnp.sqrt(v + eps)

def _scatter_add(tgt, idx, src, axis=0):
    return tgt.at[idx].add(src)

def _segment_sum(src, seg, n):
    return jax.ops.segment_sum(src, seg, n)
kernel_name = 'mk_seq_preln_d1_jaxref_r8_72a439'

def setup_inputs(seed: int=0):
    np.random.seed(seed)
    _w = jnp.asarray

    def _L0_attn_setup():
        import jax, jax.numpy as jnp
        import numpy as np
        B, N, D = (4, 512, 128)
        H, F = (16, 128)
        HD = D // H
        key = jax.random.key(seed)
        k1, k2, k3, k4, k5 = jax.random.split(key, 5)
        x = jax.random.normal(k1, (B, N, D), dtype=jnp.float32)
        W_qkv = jax.random.normal(k2, (3 * D, D), dtype=jnp.float32) * np.sqrt(2.0 / D)
        proj = jax.random.normal(k3, (H, HD, F), dtype=jnp.float32) / np.sqrt(HD)
        W_out = jax.random.normal(k4, (D, D), dtype=jnp.float32) * np.sqrt(2.0 / D)
        b_out = jnp.zeros((D,), dtype=jnp.float32)
        return {'x': x, 'W_qkv': W_qkv, 'proj': proj, 'W_out': W_out, 'b_out': b_out}
    _L0_attn_in = _L0_attn_setup()

    def _L0_ffn_setup():
        import jax, jax.numpy as jnp
        import numpy as np
        EMBED_DIM = 128
        HIDDEN_DIM = 512
        NUM_EXPERTS = 8
        TOP_K = 2
        key = jax.random.key(seed)
        ks = jax.random.split(key, 4)
        std1 = float(np.sqrt(2.0 / EMBED_DIM))
        std2 = float(np.sqrt(2.0 / HIDDEN_DIM))
        x = jax.random.normal(ks[0], (1, 256, EMBED_DIM), dtype=jnp.float32)
        w_router = jax.random.normal(ks[1], (EMBED_DIM, NUM_EXPERTS), dtype=jnp.float32) * 0.02
        w1 = jax.random.normal(ks[2], (NUM_EXPERTS, EMBED_DIM, HIDDEN_DIM), dtype=jnp.float32) * std1
        b1 = jnp.zeros((NUM_EXPERTS, HIDDEN_DIM), dtype=jnp.float32)
        w2 = jax.random.normal(ks[3], (NUM_EXPERTS, HIDDEN_DIM, EMBED_DIM), dtype=jnp.float32) * std2
        b2 = jnp.zeros((NUM_EXPERTS, EMBED_DIM), dtype=jnp.float32)
        return {'x': x, 'w_router': w_router, 'w1': w1, 'b1': b1, 'w2': w2, 'b2': b2}
    _L0_ffn_in = _L0_ffn_setup()
    _d = {'L0_attn_x': _L0_attn_in['x'], 'L0_attn_W_qkv': _L0_attn_in['W_qkv'], 'L0_attn_proj': _L0_attn_in['proj'], 'L0_attn_W_out': _L0_attn_in['W_out'], 'L0_attn_b_out': _L0_attn_in['b_out'], 'L0_ffn_w_router': _L0_ffn_in['w_router'], 'L0_ffn_w1': _L0_ffn_in['w1'], 'L0_ffn_b1': _L0_ffn_in['b1'], 'L0_ffn_w2': _L0_ffn_in['w2'], 'L0_ffn_b2': _L0_ffn_in['b2']}
    _x0 = _d['L0_attn_x']
    _d['L0_attn_x'] = jax.random.normal(jax.random.fold_in(jax.random.key(seed), 1), (8, 256, 128), dtype=_x0.dtype)
    del _x0
    return _d

def reference(L0_attn_x, L0_attn_W_qkv, L0_attn_proj, L0_attn_W_out, L0_attn_b_out, L0_ffn_w_router, L0_ffn_w1, L0_ffn_b1, L0_ffn_w2, L0_ffn_b2):

    def _L0_attn_ref(x, W_qkv, proj, W_out, b_out):
        import jax, jax.numpy as jnp
        import numpy as np
        B, N, D = (4, 512, 128)
        H, F = (16, 128)
        HD = D // H
        b, n, d = x.shape
        qkv = x @ W_qkv.T
        q, k, v = jnp.split(qkv, 3, axis=-1)
        reshp = lambda t: t.reshape(b, n, H, HD).transpose(0, 2, 1, 3)
        q, k, v = (reshp(q), reshp(k), reshp(v))
        q_p = jax.nn.elu(jnp.einsum('bhnd,hdf->bhnf', q, proj)) + 1.0
        k_p = jax.nn.elu(jnp.einsum('bhnd,hdf->bhnf', k, proj)) + 1.0
        kv = jnp.einsum('bhnf,bhnd->bhfd', k_p, v)
        attn = jnp.einsum('bhnf,bhfd->bhnd', q_p, kv)
        k_sum = k_p.sum(axis=2)
        z = 1.0 / (jnp.einsum('bhnf,bhf->bhn', q_p, k_sum) + 1e-08)
        attn = attn * z[..., None]
        attn = attn.transpose(0, 2, 1, 3).reshape(b, n, d)
        return attn @ W_out.T + b_out

    def _L0_ffn_ref(x, w_router, w1, b1, w2, b2):
        import jax, jax.numpy as jnp
        import numpy as np
        EMBED_DIM = 128
        HIDDEN_DIM = 512
        NUM_EXPERTS = 8
        TOP_K = 2
        orig_shape = x.shape
        xf = x.reshape(-1, EMBED_DIM)
        logits = xf @ w_router
        probs = jax.nn.softmax(logits, axis=-1)
        topk_w, topk_idx = jax.lax.top_k(probs, TOP_K)
        mask = jax.nn.one_hot(topk_idx, NUM_EXPERTS, dtype=xf.dtype)
        weights = jnp.sum(topk_w[..., None] * mask, axis=1)
        h = jnp.einsum('te,ieh->tih', xf, w1) + b1
        h = jax.nn.gelu(h)
        out = jnp.einsum('tih,ihe->tie', h, w2) + b2
        out = jnp.sum(out * weights[..., None], axis=1)
        return out.reshape(orig_shape)
    x = L0_attn_x
    x = x + _L0_attn_ref(_layernorm(x, axis=-1), L0_attn_W_qkv, L0_attn_proj, L0_attn_W_out, L0_attn_b_out)
    x = x + _L0_ffn_ref(_layernorm(x, axis=-1), L0_ffn_w_router, L0_ffn_w1, L0_ffn_b1, L0_ffn_w2, L0_ffn_b2)
    return x

_drawn_inputs = setup_inputs


def setup_inputs(seed=0):
    import zlib

    import numpy as np

    out = dict(_drawn_inputs(seed))
    spreads = {'L0_attn_b_out': (0.0, 0.1), 'L0_ffn_b1': (0.0, 0.377), 'L0_ffn_b2': (0.0, 0.378)}
    factors = {}
    for name, (base, spread) in spreads.items():
        noise = np.random.default_rng([zlib.crc32(name.encode()), seed]).standard_normal(out[name].shape)
        drawn = base * np.exp(spread * noise) if base else spread * noise
        out[name] = jnp.asarray(drawn.astype(out[name].dtype))
    for name, factor in factors.items():
        out[name] = (out[name] * factor).astype(out[name].dtype)
    return out
```

```python
from contextlib import ExitStack

import concourse.bass as bass
from concourse import mybir

F32 = mybir.dt.float32
F32R = mybir.dt.float32r
U32 = mybir.dt.uint32
ALU = mybir.AluOpType
ACT = mybir.ActivationFunctionType
AX = mybir.AxisListType

P = 128
D = 128
B, N = 8, 256
T = B * N // P
TPB = N // P
H, HD, F = 16, 8, 128
G = 4
HG = H // G
KS = 97
U = 16
RING = 4
FR = 8
VW = HD + 1
E, HID = 8, 512
C = HID // P
GT = 512
NG = T * P // GT
EPS = 1e-5


def build(nc, x, wqkvT, proj3, woT, bout, wr, w1, b1, w2, b2, ident, expert_no, pick, out):
    with ExitStack() as ctx:
        def sb(name, shape, dt=F32):
            return ctx.enter_context(nc.sbuf_tensor(name, shape, dt))

        def ps(name, shape):
            return ctx.enter_context(nc.psum_tensor(name, shape, F32))

        def sem(name):
            return ctx.enter_context(nc.semaphore(name))

        ident_s = sb("ident_s", [P, P])
        wqkvT_s = sb("wqkvT_s", [D, 3 * D])
        woT_s = sb("woT_s", [D, D])
        bout_s = sb("bout_s", [1, D])
        ones_row = sb("ones_row", [1, P])
        proj_raw = sb("proj_raw", [96, H * F])
        proj_st = sb("proj_st", [KS, H * F], F32R)
        wr_s = sb("wr_s", [D, E])
        w1_s = sb("w1_s", [D, E, HID])
        w2_s = sb("w2_s", [P, E, C, D])
        b1_s = sb("b1_s", [P, E, C])
        b2_s = sb("b2_s", [E, D])
        expert_no_s = sb("expert_no_s", [P, E])
        pick_s = sb("pick_s", [E, E, P])
        half_neg = sb("half_neg", [P, 2])

        x_all = sb("x_all", [P, T, D])
        xn = sb("xn", [P, 2, TPB, D])
        stats = sb("stats", [P, 2, TPB, 6])
        mv = sb("mv", [P, 2, TPB, 2])
        rstd = sb("rstd", [P, 2, TPB])
        xnT = sb("xnT", [D, 2, N])
        qk_hi = sb("qk_hi", [D, 2, T * P], F32R)
        qk_lo = sb("qk_lo", [D, 2, T * P], F32R)
        v_ext = sb("v_ext", [P, T, H, VW])
        stack = sb("stack", [KS, 2, G, 2, N], F32R)
        exps = sb("exps", [P, RING, 512])
        feats = sb("feats", [P, FR, 512])
        kv = sb("kv", [F, 2, H * VW])
        rden = sb("rden", [P, TPB * H])
        attn = sb("attn", [P, TPB, D])
        attnT = sb("attnT", [D, N])
        x1 = sb("x1", [P, T, D])
        xn2 = sb("xn2", [P, TPB, D])
        xn2T = sb("xn2T", [D, T * P])
        lmax = sb("lmax", [P, T])
        lexp = sb("lexp", [P, T, E])
        lsum = sb("lsum", [P, T])
        probs = sb("probs", [P, T, E])
        top8 = sb("top8", [P, T, 8])
        topi = sb("topi", [P, T, 8], U32)
        topf = sb("topf", [P, T, 2])
        chosen = sb("chosen", [P, 2, T, E])
        gate = sb("gate", [P, T, E])
        gateT = sb("gateT", [E, T * P])
        gel = sb("gel", [P, 4, GT])
        gs = sb("gs", [P, 4, GT])
        yT = sb("yT", [D, GT])
        res = sb("res", [P, GT // P, D])

        feat_ps = ps("feat_ps", [P, RING, 512])
        ta_ps = ps("ta_ps", [P, 2, 256])
        qk_ps = ps("qk_ps", [P, 512])
        kv_ps = ps("kv_ps", [P, 512])
        at_ps = ps("at_ps", [P, 512])
        kv_p = kv_ps[:, 0:H * VW]
        y_p = qk_ps[:, 0:TPB * D]

        consts_in = sem("consts_in")
        projw_in = sem("projw_in")
        ffw_in = sem("ffw_in")
        x_in = sem("x_in")
        set_up = sem("set_up")
        proj_split = sem("proj_split")
        ln_stats = sem("ln_stats")
        ln_mv = sem("ln_mv")
        ln_veps = sem("ln_veps")
        ln_rstd = sem("ln_rstd")
        ln_xn = sem("ln_xn")
        xnT_ps = sem("xnT_ps")
        xnT_sb = sem("xnT_sb")
        qk_mm = sem("qk_mm")
        v_mm = sem("v_mm")
        hi_done = sem("hi_done")
        lo_done = sem("lo_done")
        v_done = sem("v_done")
        stack_in = [sem("stack_in_even"), sem("stack_in_odd")]
        feat_mm = sem("feat_mm")
        exp_done = sem("exp_done")
        feat_done = sem("feat_done")
        feat_used = sem("feat_used")
        kv_sb = sem("kv_sb")
        den_done = sem("den_done")
        rden_done = sem("rden_done")
        attn_done = sem("attn_done")
        attnT_ps = sem("attnT_ps")
        attnT_sb = sem("attnT_sb")
        y_mm = sem("y_mm")
        x1_done = sem("x1_done")
        l2_stats = sem("l2_stats")
        l2_mv = sem("l2_mv")
        l2_veps = sem("l2_veps")
        l2_rstd = sem("l2_rstd")
        l2_xn = sem("l2_xn")
        xn2T_ps = sem("xn2T_ps")
        xn2T_sb = sem("xn2T_sb")
        logit_mm = sem("logit_mm")
        route = sem("route")
        lexp_done = sem("lexp_done")
        gateT_ps = sem("gateT_ps")
        gateT_sb = sem("gateT_sb")
        hid_mm = sem("hid_mm")
        gelu_done = sem("gelu_done")
        wb_mm = sem("wb_mm")
        gs_done = sem("gs_done")
        ex_mm = sem("ex_mm")
        yT_sb = sem("yT_sb")
        back_ps = sem("back_ps")
        res_done = sem("res_done")
        stored = sem("stored")
        dve_met, pool_met, sp_met = sem("dve_met"), sem("pool_met"), sem("sp_met")

        lg_all = qk_ps[:, 0:T * E].rearrange("p (t e) -> p t e", e=E)

        block = ctx.enter_context(nc.Block())

        @block.sync
        def _(sp):
            xt = x.rearrange("(t p) d -> p t d", p=P)
            sp.dma_start(x_all[:, 0:4, :], xt[:, 0:4, :]).then_inc(x_in, 16)
            sp.dma_start(ident_s[:], ident).then_inc(consts_in, 16)
            sp.dma_start(wqkvT_s[:], wqkvT).then_inc(consts_in, 16)
            sp.dma_start(woT_s[:], woT).then_inc(consts_in, 16)
            sp.dma_start(bout_s[:], bout).then_inc(consts_in, 16)
            sp.dma_start(proj_raw[:], proj3).then_inc(projw_in, 16)
            sp.dma_start(x_all[:, 4:T, :], xt[:, 4:T, :]).then_inc(x_in, 16)
            sp.dma_start(wr_s[:], wr).then_inc(consts_in, 16)
            sp.dma_start(expert_no_s[:], expert_no).then_inc(consts_in, 16)
            sp.dma_start(pick_s[:], pick).then_inc(consts_in, 16)
            sp.dma_start(w1_s[:], w1.rearrange("e d h -> d e h")).then_inc(ffw_in, 16)
            sp.dma_start(w2_s[:], w2.rearrange("e (c p) d -> p e c d", p=P)).then_inc(ffw_in, 16)
            sp.dma_start(b1_s[:], b1).then_inc(ffw_in, 16)
            sp.dma_start(b2_s[:], b2).then_inc(ffw_in, 16)

            hi_v = qk_hi[:].bitcast(F32).rearrange("p s (b n) -> p s b n", n=N)
            lo_v = qk_lo[:].bitcast(F32).rearrange("p s (b n) -> p s b n", n=N)
            st = stack[:].bitcast(F32)

            def stack_batch(b, k):
                for g in range(G):
                    rows = slice(32 * g, 32 * g + 32)
                    for at, src in ((0, hi_v), (32, lo_v), (64, hi_v)):
                        sp.dma_start(st[at:at + 32, k, g, :, :], src[rows, :, b, :]).then_inc(stack_in[k], 16)

            for b in range(2):
                sp.wait_ge(hi_done, b + 1)
                sp.wait_ge(lo_done, b + 1)
                stack_batch(b, b)
            with sp.Fori(1, B // 2) as i:
                for k in range(2):
                    sp.wait_ge(feat_mm, i * (2 * U) + (k - 1) * U)
                    sp.sem_inc(sp_met)
                    sp.wait_ge(hi_done, i * 2 + (k + 1))
                    sp.sem_inc(sp_met)
                    sp.wait_ge(lo_done, i * 2 + (k + 1))
                    sp.sem_inc(sp_met)
                    hv = qk_hi[:].bitcast(F32).rearrange("p s (i k n) -> p s i k n", n=N, k=2)
                    lv = qk_lo[:].bitcast(F32).rearrange("p s (i k n) -> p s i k n", n=N, k=2)
                    for g in range(G):
                        rows = slice(32 * g, 32 * g + 32)
                        for at, src in ((0, hv), (32, lv), (64, hv)):
                            sp.dma_start(st[at:at + 32, k, g, :, :], src[rows, :, i, k, :]).then_inc(stack_in[k], 16)
            ot = out.rearrange("(g t p) d -> g p t d", p=P, t=GT // P)
            for g in range(NG):
                sp.wait_ge(res_done, g + 1)
                sp.dma_start(ot[g], res[:]).then_inc(stored, 16)
                sp.wait_ge(stored, 16 * (g + 1))

        @block.gpsimd
        def _(pool):
            pool.memset(ones_row[:], 1.0).then_inc(set_up, 1)
            pool.memset(half_neg[:], -0.5).then_inc(set_up, 1)
            pool.memset(v_ext[:, :, :, HD:VW], 1.0).then_inc(set_up, 1)
            pool.wait_ge(set_up, 5)

            def rstd_of(b, k, m_sem, v_sem, r_sem):
                pool.wait_ge(m_sem, b * 2 + 2)
                pool.sem_inc(pool_met)
                pool.tensor_scalar(rstd[:, k, :], mv[:, k, :, 1], EPS, None, ALU.add).then_inc(v_sem, 1)
                pool.wait_ge(v_sem, b + 1)
                pool.tensor_tensor(rstd[:, k, :], rstd[:, k, :], half_neg[:], ALU.pow).then_inc(r_sem, 1)

            with pool.Fori(0, B // 2) as i:
                for k in range(2):
                    rstd_of(i * 2 + k, k, ln_mv, ln_veps, ln_rstd)
            with pool.Fori(0, B // 2) as i:
                for k in range(2):
                    rstd_of(i * 2 + k, k, l2_mv, l2_veps, l2_rstd)

        def is_first(b):
            return isinstance(b, int) and b == 0

        def pairs(eng, body):
            body(0, 0, 0)
            body(1, 0, 1)
            with eng.Fori(1, B // 2) as i:
                body(i * 2, i, 0)
                body(i * 2 + 1, i, 1)

        def batches(eng, body):
            body(0, 0, 0, True, False)
            with eng.Fori(0, B // 2 - 1) as i:
                body(i * 2 + 1, 1, i, True, True)
                body(i * 2 + 2, 0, i + 1, True, True)
            body(B - 1, 1, B // 2 - 1, True, True)
            body(B, 0, B // 2, False, True)

        x_v = x_all[:].rearrange("p (i k) d -> p i (k d)", k=2)
        x1_v = x1[:].rearrange("p (i k) d -> p i (k d)", k=2)
        xn2T_v = xn2T[:].rearrange("p (b n) -> p b n", n=N)

        def at(view, b):
            return view[:, b, :]

        @block.vector
        def _(dve):
            dve.memset(stack[96:97, :, :, :, :].bitcast(F32), 1.0).then_inc(set_up, 1)
            dve.memset(proj_st[96:97, :].bitcast(F32), 1.0).then_inc(set_up, 1)
            dve.wait_ge(projw_in, 16)
            dve.tensor_copy(proj_st[0:96, :], proj_raw[:]).then_inc(proj_split, 1)
            dve.wait_ge(proj_split, 1)
            dve.tensor_tensor(proj_st[64:96, :], proj_raw[64:96, :], proj_st[64:96, :].bitcast(F32),
                              ALU.subtract).then_inc(proj_split, 1)

            xs = x_all[:].rearrange("p (i k j) d -> p i k j d", k=2, j=TPB)
            hi_s = qk_hi[:].rearrange("p s (i k n) -> p s i k n", k=2, n=N)
            lo_s = qk_lo[:].rearrange("p s (i k n) -> p s i k n", k=2, n=N)

            def lo_part(b, i, k):
                dve.wait_ge(hi_done, b + 1)
                dve.tensor_tensor(lo_s[:, :, i, k, :], qk_ps[:].rearrange("p (s n) -> p s n", s=2),
                                  hi_s[:, :, i, k, :].bitcast(F32), ALU.subtract).then_inc(lo_done, 1)

            dve.wait_ge(x_in, 32)
            def norm(b, i, k):
                for j in range(TPB):
                    dve.bn_stats(stats[:, k, j, :], xs[:, i, k, j, :]).then_inc(ln_stats, 1)
                for j in range(TPB):
                    dve.wait_ge(ln_stats, b * 2 + (j + 1))
                    dve.sem_inc(dve_met)
                    dve.bn_aggr(mv[:, k, j, :], stats[:, k, j, :]).then_inc(ln_mv, 1)
                dve.wait_ge(ln_rstd, b + 1)
                if not is_first(b):
                    dve.wait_ge(xnT_ps, b)
                for j in range(TPB):
                    dve.tensor_scalar(xn[:, k, j, :], xs[:, i, k, j, :], mv[:, k, j, 0:1], rstd[:, k, j:j + 1],
                                      ALU.subtract, ALU.mult).then_inc(ln_xn, 1)
                lo_part(b, i, k)

            pairs(dve, norm)

            def body(b, k, r, units, tail):
                for u in range(U if units else 0):
                    dve.wait_ge(exp_done, b * U + (u + 1))
                    if not (isinstance(b, int) and b * U + u < FR):
                        dve.wait_ge(feat_used, b * U + (u + 1 - FR))
                    dve.scalar_tensor_tensor(out=feats[:, u % FR, :], in0=exps[:, u % RING, :], scalar=1.0,
                                             in1=feat_ps[:, u % RING, :], op0=ALU.min, op1=ALU.max
                                             ).then_inc(feat_done, 1)
                    if tail:
                        piece(b, k, u)
                if not units:
                    for u in range(U):
                        piece(b, k, u)

            def piece(b, k, u):
                kp = 1 - k
                ap = at_ps[:, 0:TPB * H * VW].rearrange("p (t v) -> p t v", v=VW)
                if u == 5:
                    dve.wait_ge(feat_used, b * U)
                    dve.tensor_scalar(rden[:], ap[:, :, HD], 1e-8, None, ALU.add).then_inc(den_done, 1)
                    dve.wait_ge(den_done, b)
                    dve.reciprocal(rden[:], rden[:]).then_inc(rden_done, 1)
                    dve.wait_ge(rden_done, b)
                    dve.tensor_tensor(attn[:].rearrange("p j (h d) -> p (j h) d", d=HD), ap[:, :, 0:HD],
                                      rden[:].rearrange("p (t o) -> p t o", o=1).to_broadcast((P, TPB * H, HD)),
                                      ALU.mult).then_inc(attn_done, 1)
                if u == 9:
                    dve.wait_ge(y_mm, b)
                    dve.tensor_tensor(at(x1_v, b - 1), y_p, at(x_v, b - 1), ALU.add).then_inc(x1_done, 1)
                    dve.wait_ge(x1_done, b)
                    dve.sem_inc(dve_met)
                    xv = at(x1_v, b - 1).rearrange("p (j d) -> p j d", j=TPB)
                    for j in range(TPB):
                        dve.bn_stats(stats[:, k, j, :], xv[:, j, :]).then_inc(l2_stats, 1)
                if u == 10:
                    for j in range(TPB):
                        dve.wait_ge(l2_stats, b * 2 + (j - 1))
                        dve.sem_inc(dve_met)
                        dve.bn_aggr(mv[:, kp, j, :], stats[:, k, j, :]).then_inc(l2_mv, 1)
                if u == 12:
                    dve.wait_ge(l2_rstd, b)
                    xv = at(x1_v, b - 1).rearrange("p (j d) -> p j d", j=TPB)
                    for j in range(TPB):
                        dve.tensor_scalar(xn2[:, j, :], xv[:, j, :], mv[:, kp, j, 0:1], rstd[:, kp, j:j + 1],
                                          ALU.subtract, ALU.mult).then_inc(l2_xn, 1)

            batches(dve, body)

            dve.wait_ge(logit_mm, T)
            step = 0

            def link(ins):
                nonlocal step
                step += 1
                ins.then_inc(route, 1)
                dve.wait_ge(route, step)
            link(dve.tensor_reduce(lmax[:], lg_all, AX.X, ALU.max))
            bc = lambda t: t.rearrange("p (t o) -> p t o", o=1).to_broadcast((P, T, E))
            link(dve.tensor_tensor(lexp[:], lg_all, bc(lmax[:]), ALU.subtract))
            dve.wait_ge(lexp_done, 1)
            link(dve.tensor_reduce(lsum[:], lexp[:], AX.X, ALU.add))
            link(dve.reciprocal(lsum[:], lsum[:]))
            link(dve.tensor_tensor(probs[:], lexp[:], bc(lsum[:]), ALU.mult))
            for t in range(T):
                ins = dve.max(top8[:, t, :], probs[:, t, :])
            link(ins)
            for t in range(T):
                ins = dve.max_index(topi[:, t, :], top8[:, t, :], probs[:, t, :])
            link(ins)
            link(dve.tensor_copy(topf[:], topi[:, :, 0:2]))
            en = expert_no_s[:].rearrange("p (o e) -> p o e", o=1).to_broadcast((P, T, E))
            for r in range(2):
                link(dve.tensor_tensor(chosen[:, r, :, :], en,
                                       topf[:, :, r:r + 1].to_broadcast((P, T, E)), ALU.is_equal))
            link(dve.tensor_tensor(chosen[:, 0, :, :], chosen[:, 0, :, :], chosen[:, 1, :, :], ALU.add))
            link(dve.tensor_tensor(gate[:], probs[:], chosen[:, 0, :, :], ALU.mult))

            dve.wait_ge(ffw_in, 64)
            for g in range(NG):
                n = g * E
                for e in range(E):
                    for c in range(C):
                        m = (n + e) * C + c
                        dve.wait_ge(gelu_done, m + 1)
                        dve.wait_ge(wb_mm, n + e + 1)
                        if m >= 4:
                            dve.wait_ge(ex_mm, m - 3)
                        dve.tensor_tensor(gs[:, c, :], gel[:, c, :], at_ps[:], ALU.mult).then_inc(gs_done, 1)
                dve.wait_ge(back_ps, g + 1)
                if g:
                    dve.wait_ge(stored, 16 * g)
                dve.tensor_tensor(res[:].rearrange("p t d -> p (t d)"), kv_ps[:],
                                  x1[:, 4 * g:4 * g + 4, :].rearrange("p t d -> p (t d)"),
                                  ALU.add).then_inc(res_done, 1)

        @block.scalar
        def _(act):
            hi_s = qk_hi[:].rearrange("p s (i k n) -> p s i k n", k=2, n=N)
            v_s = v_ext[:].rearrange("p (i k j) h v -> p i k (j h) v", k=2, j=TPB)
            with act.Fori(0, B // 2) as i:
                for k in range(2):
                    b = i * 2 + k
                    act.wait_ge(xnT_ps, b + 1)
                    act.copy(xnT[:, k, :], ta_ps[:, 0, :]).then_inc(xnT_sb, 1)
                    act.wait_ge(qk_mm, b + 1)
                    act.copy(hi_s[:, :, i, k, :], qk_ps[:].rearrange("p (s n) -> p s n", s=2)).then_inc(hi_done, 1)
                    act.wait_ge(v_mm, b + 1)
                    act.copy(v_s[:, i, k, :, 0:HD],
                             ta_ps[:, 0, :].rearrange("p (t d) -> p t d", d=HD)).then_inc(v_done, 1)

            def body(b, k, r, units, tail):
                for u in range(U if units else 0):
                    if u == 12:
                        act.wait_ge(feat_used, b * U + 8)
                        act.copy(kv[:, k, :], kv_p).then_inc(kv_sb, 1)
                    act.wait_ge(feat_mm, b * U + (u + 1))
                    act.activation(exps[:, u % RING, :], feat_ps[:, u % RING, :], ACT.Exp,
                                   bias=-1.0).then_inc(exp_done, 1)
                    if tail:
                        piece(b, k, u)
                if not units:
                    for u in range(U):
                        piece(b, k, u)

            def piece(b, k, u):
                if u == 9:
                    act.wait_ge(attnT_ps, b)
                    act.copy(attnT[:], ta_ps[:, 1, :]).then_inc(attnT_sb, 1)
                if u == 15:
                    act.wait_ge(xn2T_ps, b)
                    act.copy(at(xn2T_v, b - 1), ta_ps[:, 1, :]).then_inc(xn2T_sb, 1)

            batches(act, body)
            act.wait_ge(route, 2)
            act.activation(lexp[:], lexp[:], ACT.Exp).then_inc(lexp_done, 1)
            act.wait_ge(ffw_in, 64)
            for g in range(NG):
                act.wait_ge(gateT_ps, g + 1)
                act.copy(gateT[:, g * GT:(g + 1) * GT], ta_ps[0:E, :, :].rearrange("p a n -> p (a n)")
                         ).then_inc(gateT_sb, 1)
            for g in range(NG):
                for e in range(E):
                    for c in range(C):
                        m = (g * E + e) * C + c
                        act.wait_ge(hid_mm, m + 1)
                        if m >= 4:
                            act.wait_ge(gs_done, m - 3)
                        act.activation(gel[:, c, :], feat_ps[:, c, :], ACT.Gelu_apprx_tanh,
                                       bias=b1_s[:, e, c:c + 1]).then_inc(gelu_done, 1)
                act.wait_ge(ex_mm, (g + 1) * E * C)
                act.copy(yT[:], qk_ps[:]).then_inc(yT_sb, 1)

        @block.tensor
        def _(pe):
            pe.wait_ge(consts_in, 16 * 7)
            pe.wait_ge(set_up, 5)
            def project(b, i, k):
                pe.wait_ge(ln_xn, b * 2 + 2)
                if not is_first(b):
                    pe.wait_ge(v_done, b)
                for j in range(TPB):
                    mm = pe.transpose(ta_ps[:, 0, j * P:(j + 1) * P], xn[:, k, j, :], ident_s[:])
                mm.then_inc(xnT_ps, 1)
                pe.wait_ge(xnT_sb, b + 1)
                if not is_first(b):
                    pe.wait_ge(lo_done, b)
                for s in range(2):
                    mm = pe.matmul(qk_ps[:, s * N:(s + 1) * N], wqkvT_s[:, s * D:(s + 1) * D], xnT[:, k, :],
                                   start=True, stop=True)
                mm.then_inc(qk_mm, 1)
                for j in range(TPB):
                    mm = pe.matmul(ta_ps[:, 0, j * P:(j + 1) * P], xnT[:, k, j * P:(j + 1) * P],
                                   wqkvT_s[:, 2 * D:3 * D], start=True, stop=True)
                mm.then_inc(v_mm, 1)

            pairs(pe, project)
            pe.wait_ge(proj_split, 2)
            v_t = v_ext[:].rearrange("p (b j) h v -> p b (j h v)", j=TPB)

            def feature(b, k, u):
                slot = u % RING
                if u < 8:
                    g, j = u // 2, u % 2
                    mm = pe.matmul(feat_ps[:, slot, :], stack[:, k, g, 1, j * P:(j + 1) * P],
                                   proj_st[:, g * 512:(g + 1) * 512], start=True, stop=True)
                else:
                    for h in (2 * (u - 8), 2 * (u - 8) + 1):
                        mm = pe.matmul(feat_ps[:, slot, (h % 2) * N:(h % 2 + 1) * N],
                                       proj_st[:, h * F:(h + 1) * F], stack[:, k, h // HG, 0, :],
                                       start=True, stop=True)
                mm.then_inc(feat_mm, 1)

            def kv_group(b, k, g):
                for h in range(HG * g, HG * g + HG):
                    for j in range(TPB):
                        f = feats[:, (2 * g + j) % FR, (h % HG) * F:(h % HG + 1) * F]
                        v0 = (j * H + h) * VW
                        mm = pe.matmul(kv_ps[:, h * VW:(h + 1) * VW], f, v_t[:, b, v0:v0 + VW],
                                       start=(j == 0), stop=(j == TPB - 1))
                mm.then_inc(feat_used, 2)

            def attn_unit(k, m):
                for h in (2 * m, 2 * m + 1):
                    for j in range(TPB):
                        f = feats[:, (8 + m) % FR, (h % 2) * N + j * P:(h % 2) * N + (j + 1) * P]
                        o = (j * H + h) * VW
                        mm = pe.matmul(at_ps[:, o:o + VW], f, kv[:, k, h * VW:(h + 1) * VW], start=True, stop=True)
                mm.then_inc(feat_used, 1)

            def body(b, k, r, units, tail):
                if units:
                    pe.wait_ge(stack_in[k], r * (12 * 16) + 12 * 16)
                for u in range(U):
                    if units:
                        if not (isinstance(b, int) and b * U + u < RING):
                            pe.wait_ge(feat_done, b * U + (u + 1 - RING))
                        feature(b, k, u)
                        if u in (5, 7, 9, 11):
                            g = (u - 5) // 2
                            pe.wait_ge(feat_done, b * U + (2 * g + 2))
                            kv_group(b, k, g)
                        if u >= 12:
                            if u == 12:
                                pe.wait_ge(kv_sb, b + 1)
                                if not (isinstance(b, int) and b == 0):
                                    pe.wait_ge(attn_done, b)
                            pe.wait_ge(feat_done, b * U + (u - 3))
                            attn_unit(k, u - 12)
                    if tail and u < 4:
                        pe.wait_ge(feat_done, b * U + (u - 3))
                        attn_unit(1 - k, u + 4)
                    if tail and u == 8:
                        pe.wait_ge(attn_done, b)
                        if not units:
                            pe.wait_ge(xn2T_sb, b - 1)
                        for j in range(TPB):
                            mm = pe.transpose(ta_ps[:, 1, j * P:(j + 1) * P], attn[:, j, :], ident_s[:])
                        mm.then_inc(attnT_ps, 1)
                    if tail and u == 11:
                        pe.wait_ge(attnT_sb, b)
                        for j in range(TPB):
                            yo = qk_ps[:, j * D:(j + 1) * D]
                            pe.matmul(yo, attnT[:, j * P:(j + 1) * P], woT_s[:], start=True, stop=False)
                            mm = pe.matmul(yo, ones_row[:], bout_s[:], start=False, stop=True)
                        mm.then_inc(y_mm, 1)
                    if tail and u == 15:
                        pe.wait_ge(l2_xn, b * 2)
                        for j in range(TPB):
                            mm = pe.transpose(ta_ps[:, 1, j * P:(j + 1) * P], xn2[:, j, :], ident_s[:])
                        mm.then_inc(xn2T_ps, 1)

            batches(pe, body)
            pe.wait_ge(xn2T_sb, B)
            for t in range(T):
                mm = pe.matmul(qk_ps[:, t * E:(t + 1) * E], xn2T[:, t * P:(t + 1) * P], wr_s[:], start=True, stop=True)
                mm.then_inc(logit_mm, 1)
            pe.wait_ge(route, 12)
            for g in range(NG):
                if g:
                    pe.wait_ge(gateT_sb, g)
                for t in range(4):
                    mm = pe.transpose(ta_ps[0:E, t // 2, (t % 2) * P:(t % 2 + 1) * P], gate[:, 4 * g + t, :], ident_s[:])
                mm.then_inc(gateT_ps, 1)
            pe.wait_ge(gateT_sb, NG)
            pe.wait_ge(ffw_in, 64)

            def up(m):
                g, e, c = m // (E * C), m // C % E, m % C
                if m >= 4:
                    pe.wait_ge(gelu_done, m - 3)
                pe.matmul(feat_ps[:, c, :], w1_s[:, e, c * P:(c + 1) * P], xn2T[:, g * GT:(g + 1) * GT],
                          start=True, stop=True).then_inc(hid_mm, 1)

            def down(m):
                g, e, c = m // (E * C), m // C % E, m % C
                if m % (E * C) == 0:
                    if g:
                        pe.wait_ge(yT_sb, g)
                    pe.matmul(qk_ps[:], b2_s[:], gateT[:, g * GT:(g + 1) * GT], start=True, stop=False)
                if c == 0:
                    if m:
                        pe.wait_ge(gs_done, m)
                    pe.matmul(at_ps[:], pick_s[:, e, :], gateT[:, g * GT:(g + 1) * GT], start=True,
                              stop=True).then_inc(wb_mm, 1)
                pe.wait_ge(gs_done, m + 1)
                pe.matmul(qk_ps[:], w2_s[:, e, c, :], gs[:, c, :], start=False,
                          stop=(m % (E * C) == E * C - 1)).then_inc(ex_mm, 1)

            M = NG * E * C
            for m in range(M + 4):
                if m < M:
                    up(m)
                if m >= 4:
                    down(m - 4)
                    if (m - 3) % (E * C) == 0:
                        g = (m - 3) // (E * C) - 1
                        pe.wait_ge(yT_sb, g + 1)
                        if g:
                            pe.wait_ge(res_done, g)
                        for t in range(4):
                            mm = pe.transpose(kv_ps[:, t * P:(t + 1) * P], yT[:, t * P:(t + 1) * P], ident_s[:])
                        mm.then_inc(back_ps, 1)


_OUT = (B, N, D)


def kernel(L0_attn_x, L0_attn_W_qkv, L0_attn_proj, L0_attn_W_out, L0_attn_b_out, L0_ffn_w_router,
           L0_ffn_w1, L0_ffn_b1, L0_ffn_w2, L0_ffn_b2):
    import numpy as np
    import concourse.bacc as bacc
    from concourse.bass_utils import run_bass_kernel_spmd

    proj = np.asarray(L0_attn_proj)
    proj3 = np.zeros((3, HG, HD, G, HG, F), proj.dtype)
    for j in range(HG):
        proj3[:, j, :, :, j, :] = proj.reshape(G, HG, HD, F)[:, j].transpose(1, 0, 2)
    pick = np.zeros((E, E, P), np.float32)
    for e in range(E):
        pick[e, e, :] = 1.0
    arrays = {
        "x": np.asarray(L0_attn_x).reshape(T * P, D),
        "wqkvT": np.asarray(L0_attn_W_qkv).T,
        "proj3": proj3.reshape(96, H * F),
        "woT": np.asarray(L0_attn_W_out).T,
        "bout": np.asarray(L0_attn_b_out).reshape(1, D),
        "wr": np.asarray(L0_ffn_w_router),
        "w1": np.asarray(L0_ffn_w1),
        "b1": np.asarray(L0_ffn_b1).reshape(E, C, P).transpose(2, 0, 1),
        "w2": np.asarray(L0_ffn_w2),
        "b2": np.asarray(L0_ffn_b2),
        "ident": np.eye(P, dtype=np.float32),
        "expert_no": np.tile(np.arange(E, dtype=np.float32), (P, 1)),
        "pick": pick,
    }
    arrays = {k: np.ascontiguousarray(v) for k, v in arrays.items()}
    nc = bacc.Bacc("TRN2", target_bir_lowering=False, num_devices=1)
    args = [nc.dram_tensor(k, v.shape, mybir.dt.from_np(v.dtype), kind="ExternalInput").ap() for k, v in arrays.items()]
    out = nc.dram_tensor("out", (T * P, D), F32, kind="ExternalOutput").ap()
    build(nc, *args, out)
    r = run_bass_kernel_spmd(nc, [arrays], core_ids=[0])
    return r.results[0]["out"].reshape(B, N, D)
```

```python
from contextlib import ExitStack

import concourse.bass as bass
from concourse import mybir

F32 = mybir.dt.float32
F32R = mybir.dt.float32r
U32 = mybir.dt.uint32
ALU = mybir.AluOpType
ACT = mybir.ActivationFunctionType
AX = mybir.AxisListType

P = 128
D = 128
B, N = 8, 256
T = B * N // P
TPB = N // P
H, HD, F = 16, 8, 128
G = 4
HG = H // G
KS = 97
U = 16
RING = 4
FR = 8
SLOT = 16
CH = 4
TC = T // CH
E, HID = 8, 512
C = HID // P
GT = 512
NG = T * P // GT
EPS = 1e-5
CONSTS = 7


def build(nc, x, wqkvT, proj3, woT, bout, wr, w1, b1, w2, b2, ident, expert_no, pick, out):
    with ExitStack() as ctx:
        def sb(name, shape, dt=F32):
            return ctx.enter_context(nc.sbuf_tensor(name, shape, dt))

        def ps(name, shape):
            return ctx.enter_context(nc.psum_tensor(name, shape, F32))

        def sem(name):
            return ctx.enter_context(nc.semaphore(name))

        ident_s = sb("ident_s", [P, P])
        wqkvT_s = sb("wqkvT_s", [D, 3 * D])
        woT_s = sb("woT_s", [D, D])
        bout_s = sb("bout_s", [P, D])
        ones_row = sb("ones_row", [1, P])
        proj_raw = sb("proj_raw", [96, H * F])
        proj_st = sb("proj_st", [KS, H * F], F32R)
        wr_s = sb("wr_s", [D, E])
        w1_s = sb("w1_s", [D, E, HID])
        w2_s = sb("w2_s", [P, E, C, D])
        b1_s = sb("b1_s", [P, E, C])
        b2_s = sb("b2_s", [E, D])
        expert_no_s = sb("expert_no_s", [P, E])
        pick_s = sb("pick_s", [E, E, P])
        half_neg = sb("half_neg", [P, TC])
        eps_col = sb("eps_col", [P, 1])

        x_all = sb("x_all", [P, T, D])
        xb = sb("xb", [P, T, D])
        xn = sb("xn", [P, 2, TC, D])
        stats = sb("stats", [P, T, 6])
        mv = sb("mv", [P, T, 2])
        rstd = sb("rstd", [P, T])
        xnT = sb("xnT", [D, 2, TC * P])
        qk_hi = sb("qk_hi", [D, 2, T * P], F32R)
        qk_lo = sb("qk_lo", [D, 2, T * P], F32R)
        v_all = sb("v_all", [P, T, D])
        v_z = sb("v_z", [P, 2, TPB, H, 2 * SLOT])
        stack = sb("stack", [KS, 2, G, 2, N], F32R)
        exps = sb("exps", [P, RING, 512])
        feats = sb("feats", [P, FR, 512])
        kvT = sb("kvT", [P, 2 * F])
        kv_z = sb("kv_z", [F, H, 2 * SLOT])
        atT = sb("atT", [P, 2 * N])
        rden = sb("rden", [P, TPB * H])
        attn = sb("attn", [P, TPB, D])
        attnT = sb("attnT", [D, N])
        stats2 = sb("stats2", [P, TPB, 6])
        mv2 = sb("mv2", [P, TPB, 2])
        rstd2 = sb("rstd2", [P, TPB])
        x1_cur = sb("x1_cur", [P, 2, TPB, D])
        x1 = x_all
        xn2 = sb("xn2", [P, TPB, D])
        xn2T = sb("xn2T", [D, T * P])
        lmax = sb("lmax", [P, T])
        lexp = sb("lexp", [P, T, E])
        lsum = sb("lsum", [P, T])
        probs = sb("probs", [P, T, E])
        top8 = sb("top8", [P, T, 8])
        topi = sb("topi", [P, T, 8], U32)
        topf = sb("topf", [P, T, 2])
        chosen = sb("chosen", [P, 2, T, E])
        gate = sb("gate", [P, T, E])
        gateT = sb("gateT", [E, T * P])
        gel = exps
        gs = feats
        yT = atT
        res = sb("res", [P, GT // P, D])

        feat_ps = ps("feat_ps", [P, RING, 512])
        kv_ps = ps("kv_ps", [P, 512])
        at_ps = ps("at_ps", [P, 512])
        mix_ps = ps("mix_ps", [P, 512])
        x_ps = ps("x_ps", [P, 512])

        consts_in = sem("consts_in")
        projw_in = sem("projw_in")
        ffw_in = sem("ffw_in")
        x_in = [sem("x_in_first"), sem("x_in_rest")]
        pool_set, dve_set = sem("pool_set"), sem("dve_set")
        proj_split = sem("proj_split")
        ln_stats = sem("ln_stats")
        ln_mv = sem("ln_mv")
        ln_veps = sem("ln_veps")
        ln_rstd = sem("ln_rstd")
        ln_xn = sem("ln_xn")
        xb_done = sem("xb_done")
        xnT_ps = sem("xnT_ps")
        xnT_sb = sem("xnT_sb")
        qk_mm = sem("qk_mm")
        v_mm = sem("v_mm")
        hi_done = sem("hi_done")
        lo_done = sem("lo_done")
        v_done = sem("v_done")
        feat_mm = sem("feat_mm")
        exp_done = sem("exp_done")
        feat_done = sem("feat_done")
        feat_used = sem("feat_used")
        vz_done = sem("vz_done")
        kvT_sb = sem("kvT_sb")
        kvz_ps = sem("kvz_ps")
        kvz_sb = sem("kvz_sb")
        atT_sb = sem("atT_sb")
        atok_ps = sem("atok_ps")
        den_done = sem("den_done")
        rden_done = sem("rden_done")
        attn_done = sem("attn_done")
        attnT_ps = sem("attnT_ps")
        attnT_sb = sem("attnT_sb")
        y_mm = sem("y_mm")
        x1_done = sem("x1_done")
        x1_kept = sem("x1_kept")
        l2_stats = sem("l2_stats")
        l2_mv = sem("l2_mv")
        l2_veps = sem("l2_veps")
        l2_rstd = sem("l2_rstd")
        l2_xn = sem("l2_xn")
        xn2T_ps = sem("xn2T_ps")
        xn2T_sb = sem("xn2T_sb")
        logit_mm = sem("logit_mm")
        route = sem("route")
        lexp_done = sem("lexp_done")
        gateT_ps = sem("gateT_ps")
        gateT_sb = sem("gateT_sb")
        hid_mm = sem("hid_mm")
        gelu_done = sem("gelu_done")
        wb_mm = sem("wb_mm")
        gs_done = sem("gs_done")
        ex_mm = sem("ex_mm")
        yT_sb = sem("yT_sb")
        back_ps = sem("back_ps")
        res_done = sem("res_done")
        stored = sem("stored")
        dve_met = sem("dve_met")
        pool_met = sem("pool_met")
        sp_met = sem("sp_met")
        stack_in = [sem("stack_in_even"), sem("stack_in_odd")]

        lg_all = mix_ps[:, 0:T * E].rearrange("p (t e) -> p t e", e=E)

        block = ctx.enter_context(nc.Block())

        @block.sync
        def _(sp):
            xt = x.rearrange("(t p) d -> p t d", p=P)
            sp.dma_start(x_all[:, 0:4, :], xt[:, 0:4, :]).then_inc(x_in[0], 16)
            sp.dma_start(x_all[:, 4:T, :], xt[:, 4:T, :]).then_inc(x_in[1], 16)
            sp.dma_start(ident_s[:], ident).then_inc(consts_in, 16)
            sp.dma_start(wqkvT_s[:], wqkvT).then_inc(consts_in, 16)
            sp.dma_start(woT_s[:], woT).then_inc(consts_in, 16)
            sp.dma_start(bout_s[:], bout).then_inc(consts_in, 16)
            sp.dma_start(proj_raw[:], proj3).then_inc(projw_in, 16)
            sp.dma_start(wr_s[:], wr).then_inc(consts_in, 16)
            sp.dma_start(expert_no_s[:], expert_no).then_inc(consts_in, 16)
            sp.dma_start(pick_s[:], pick).then_inc(consts_in, 16)
            sp.dma_start(w1_s[:], w1.rearrange("e d h -> d e h")).then_inc(ffw_in, 16)
            sp.dma_start(w2_s[:], w2.rearrange("e (c p) d -> p e c d", p=P)).then_inc(ffw_in, 16)
            sp.dma_start(b1_s[:], b1).then_inc(ffw_in, 16)
            sp.dma_start(b2_s[:], b2).then_inc(ffw_in, 16)

            hi_v = qk_hi[:].bitcast(F32).rearrange("p s (b n) -> p s b n", n=N)
            lo_v = qk_lo[:].bitcast(F32).rearrange("p s (b n) -> p s b n", n=N)
            st = stack[:].bitcast(F32)

            def stack_batch(b, k, hi_rows, lo_rows):
                for g in range(G):
                    rows = slice(32 * g, 32 * g + 32)
                    for at, src in ((0, hi_rows), (32, lo_rows), (64, hi_rows)):
                        sp.dma_start(st[at:at + 32, k, g, :, :], src[rows]).then_inc(stack_in[k], 16)

            sp.wait_ge(hi_done, 1)
            sp.wait_ge(lo_done, 1)
            for b in range(2):
                stack_batch(b, b, hi_v[:, :, b, :], lo_v[:, :, b, :])
            hi_k = qk_hi[:].bitcast(F32).rearrange("p s (i k n) -> p s i k n", n=N, k=2)
            lo_k = qk_lo[:].bitcast(F32).rearrange("p s (i k n) -> p s i k n", n=N, k=2)
            with sp.Fori(1, B // 2) as i:
                for k in range(2):
                    sp.wait_ge(feat_mm, i * (2 * U) + (k - 1) * U)
                    sp.sem_inc(sp_met)
                    sp.wait_ge(hi_done, i + 1)
                    sp.sem_inc(sp_met)
                    sp.wait_ge(lo_done, i + 1)
                    sp.sem_inc(sp_met)
                    stack_batch(i, k, hi_k[:, :, i, k, :], lo_k[:, :, i, k, :])
            ot = out.rearrange("(g t p) d -> g p t d", p=P, t=GT // P)
            for g in range(NG):
                sp.wait_ge(res_done, g + 1)
                sp.dma_start(ot[g], res[:]).then_inc(stored, 16)
                sp.wait_ge(stored, 16 * (g + 1))

        def batches(eng, body):
            body(0, 0, 0, True, False, False)
            body(1, 1, 0, True, True, False)
            with eng.Fori(0, B // 2 - 1) as i:
                body(i * 2 + 2, 0, i + 1, True, True, True)
                body(i * 2 + 3, 1, i + 1, True, True, True)
            body(B, 0, B // 2, False, True, True)
            body(B + 1, 1, B // 2, False, False, True)

        def is_first(b):
            return isinstance(b, int) and b == 0

        xb_v = xb[:].rearrange("p (b j) d -> p b (j d)", j=TPB)
        x1_v = x1[:].rearrange("p (b j) d -> p b (j d)", j=TPB)
        xn2T_v = xn2T[:].rearrange("p (b n) -> p b n", n=N)

        @block.gpsimd
        def _(pool):
            pool.memset(ones_row[:], 1.0).then_inc(pool_set, 1)
            pool.memset(half_neg[:], -0.5).then_inc(pool_set, 1)

            for c in range(CH):
                ts = slice(c * TC, (c + 1) * TC)
                pool.wait_ge(ln_mv, TC * (c + 1))
                pool.tensor_scalar(rstd[:, ts], mv[:, ts, 1], EPS, None, ALU.add).then_inc(ln_veps, 1)
                pool.wait_ge(ln_veps, c + 1)
                pool.wait_ge(pool_set, 2)
                pool.tensor_tensor(rstd[:, ts], rstd[:, ts], half_neg[:], ALU.pow).then_inc(ln_rstd, 1)
            pool.wait_ge(consts_in, 16 * CONSTS)
            pool.tensor_tensor(xb[:], x_all[:], bout_s[:].rearrange("p (o d) -> p o d", o=1).to_broadcast((P, T, D)),
                               ALU.add).then_inc(xb_done, 1)

            v_src = v_all[:].rearrange("p (b j) (s l h d) -> p b l (j s) h d", j=TPB, s=2, l=2, h=HG)

            def body(b, k, r, units, tail, norm):
                if units:
                    pool.wait_ge(v_done, r + 1)
                    pool.sem_inc(pool_met)
                    if not (isinstance(b, int) and b < 2):
                        pool.wait_ge(feat_used, b * U - (2 * U - 8))
                        pool.sem_inc(pool_met)
                    for l in range(2):
                        dst = v_z[:, k, :, :, :].rearrange("p j (s l h) c -> p l (j s) h c", s=2, l=2)
                        pool.tensor_copy(dst[:, l, :, :, SLOT * l:SLOT * l + HD], v_src[:, b, l]).then_inc(vz_done, 1)
                if norm:
                    pool.wait_ge(x1_done, b - 1)
                    pool.sem_inc(pool_met)
                    pool.tensor_copy(x1_v[:, b - 2, :], x1_cur[:, k].rearrange("p j d -> p (j d)")).then_inc(x1_kept, 1)
                    pool.wait_ge(l2_mv, b * 2 - 2)
                    pool.sem_inc(pool_met)
                    pool.tensor_scalar(rstd2[:], mv2[:, :, 1], EPS, None, ALU.add).then_inc(l2_veps, 1)
                    pool.wait_ge(l2_veps, b - 1)
                    pool.tensor_tensor(rstd2[:], rstd2[:], half_neg[:, 0:TPB], ALU.pow).then_inc(l2_rstd, 1)
                    pool.wait_ge(l2_rstd, b - 1)
                    pool.sem_inc(pool_met)
                    for j in range(TPB):
                        pool.tensor_scalar(xn2[:, j, :], x1_cur[:, k, j, :], mv2[:, j, 0:1], rstd2[:, j:j + 1],
                                           ALU.subtract, ALU.mult).then_inc(l2_xn, 1)

            pool.wait_ge(dve_set, 6)
            batches(pool, body)

        @block.vector
        def _(dve):
            dve.memset(stack[96:97, :, :, :, :].bitcast(F32), 1.0).then_inc(dve_set, 1)

            def stats_of(c):
                for t in range(c * TC, (c + 1) * TC):
                    dve.bn_stats(stats[:, t, :], x_all[:, t, :]).then_inc(ln_stats, 1)
                dve.wait_ge(ln_stats, (c + 1) * TC)
                for t in range(c * TC, (c + 1) * TC):
                    dve.bn_aggr(mv[:, t, :], stats[:, t, :]).then_inc(ln_mv, 1)

            def norm_of(c):
                dve.wait_ge(ln_rstd, c + 1)
                if c >= 2:
                    dve.wait_ge(xnT_ps, c - 1)
                for j in range(TC):
                    t = c * TC + j
                    dve.tensor_scalar(xn[:, c % 2, j, :], x_all[:, t, :], mv[:, t, 0:1], rstd[:, t:t + 1],
                                      ALU.subtract, ALU.mult).then_inc(ln_xn, 1)

            def lo_of(c):
                dve.wait_ge(hi_done, c + 1)
                cs = slice(c * TC * P, (c + 1) * TC * P)
                dve.tensor_tensor(qk_lo[:, :, cs], feat_ps[:, 2 * (c % 2):2 * (c % 2) + 2, :],
                                  qk_hi[:, :, cs].bitcast(F32), ALU.subtract).then_inc(lo_done, 1)

            dve.wait_ge(x_in[0], 16)
            stats_of(0)
            dve.wait_ge(x_in[1], 16)
            stats_of(1)
            norm_of(0)
            stats_of(2)
            norm_of(1)
            stats_of(3)
            norm_of(2)
            lo_of(0)
            norm_of(3)
            dve.memset(v_z[:], 0.0).then_inc(dve_set, 1)
            dve.memset(kv_z[:], 0.0).then_inc(dve_set, 1)
            dve.memset(proj_st[96:97, :].bitcast(F32), 1.0).then_inc(dve_set, 1)
            dve.wait_ge(projw_in, 16)
            dve.tensor_copy(proj_st[0:96, :], proj_raw[:]).then_inc(proj_split, 1)
            dve.wait_ge(proj_split, 1)
            dve.tensor_tensor(proj_st[64:96, :], proj_raw[64:96, :], proj_st[64:96, :].bitcast(F32),
                              ALU.subtract).then_inc(proj_split, 1)
            dve.wait_ge(dve_set, 2)
            for l in range(2):
                ones_at = v_z[:].rearrange("p k j (s l h) c -> p l (k j s) h c", s=2, l=2)
                dve.memset(ones_at[:, l, :, :, SLOT * l + HD], 1.0).then_inc(dve_set, 1)
            for c in range(1, CH):
                lo_of(c)

            by_head = mix_ps[:].rearrange("p (t c) -> p t c", c=SLOT)

            def body(b, k, r, units, tail, norm):
                for u in range(U):
                    if units:
                        dve.wait_ge(exp_done, b * U + (u + 1))
                        if not (isinstance(b, int) and b * U + u < FR):
                            dve.wait_ge(feat_used, b * U + (u + 1 - FR))
                        dve.scalar_tensor_tensor(out=feats[:, u % FR, :], in0=exps[:, u % RING, :], scalar=1.0,
                                                 in1=feat_ps[:, u % RING, :], op0=ALU.min, op1=ALU.max
                                                 ).then_inc(feat_done, 1)
                    if norm and u == 0:
                        dve.wait_ge(x1_done, b - 1)
                        dve.sem_inc(dve_met)
                        for j in range(TPB):
                            dve.bn_stats(stats2[:, j, :], x1_cur[:, k, j, :]).then_inc(l2_stats, 1)
                    if norm and u == 1:
                        dve.wait_ge(l2_stats, b * 2 - 2)
                        dve.sem_inc(dve_met)
                        for j in range(TPB):
                            dve.bn_aggr(mv2[:, j, :], stats2[:, j, :]).then_inc(l2_mv, 1)
                    if tail and u == 6:
                        dve.wait_ge(atok_ps, b)
                        dve.tensor_scalar(rden[:], by_head[:, :, HD], 1e-8, None, ALU.add).then_inc(den_done, 1)
                        dve.wait_ge(den_done, b)
                        dve.reciprocal(rden[:], rden[:]).then_inc(rden_done, 1)
                        dve.wait_ge(rden_done, b)
                        dve.tensor_tensor(attn[:].rearrange("p j (h d) -> p (j h) d", d=HD), by_head[:, :, 0:HD],
                                          rden[:].rearrange("p (t o) -> p t o", o=1).to_broadcast((P, TPB * H, HD)),
                                          ALU.mult).then_inc(attn_done, 1)
                    if tail and u == 12:
                        dve.wait_ge(y_mm, b)
                        dve.tensor_tensor(x1_cur[:, 1 - k].rearrange("p j d -> p (j d)"), mix_ps[:, 0:TPB * D], xb_v[:, b - 1, :],
                                          ALU.add).then_inc(x1_done, 1)

            dve.wait_ge(xb_done, 1)
            batches(dve, body)

            dve.wait_ge(logit_mm, T)
            step = 0

            def link(ins):
                nonlocal step
                step += 1
                ins.then_inc(route, 1)
                dve.wait_ge(route, step)
            link(dve.tensor_reduce(lmax[:], lg_all, AX.X, ALU.max))
            bc = lambda t: t.rearrange("p (t o) -> p t o", o=1).to_broadcast((P, T, E))
            link(dve.tensor_tensor(lexp[:], lg_all, bc(lmax[:]), ALU.subtract))
            dve.wait_ge(lexp_done, 1)
            link(dve.tensor_reduce(lsum[:], lexp[:], AX.X, ALU.add))
            link(dve.reciprocal(lsum[:], lsum[:]))
            link(dve.tensor_tensor(probs[:], lexp[:], bc(lsum[:]), ALU.mult))
            for t in range(T):
                ins = dve.max(top8[:, t, :], probs[:, t, :])
            link(ins)
            for t in range(T):
                ins = dve.max_index(topi[:, t, :], top8[:, t, :], probs[:, t, :])
            link(ins)
            link(dve.tensor_copy(topf[:], topi[:, :, 0:2]))
            en = expert_no_s[:].rearrange("p (o e) -> p o e", o=1).to_broadcast((P, T, E))
            for r in range(2):
                link(dve.tensor_tensor(chosen[:, r, :, :], en,
                                       topf[:, :, r:r + 1].to_broadcast((P, T, E)), ALU.is_equal))
            link(dve.tensor_tensor(chosen[:, 0, :, :], chosen[:, 0, :, :], chosen[:, 1, :, :], ALU.add))
            link(dve.tensor_tensor(gate[:], probs[:], chosen[:, 0, :, :], ALU.mult))

            dve.wait_ge(ffw_in, 64)
            dve.wait_ge(x1_kept, B)
            for g in range(NG):
                n = g * E
                for e in range(E):
                    for c in range(C):
                        m = (n + e) * C + c
                        dve.wait_ge(gelu_done, m + 1)
                        dve.wait_ge(wb_mm, n + e + 1)
                        if m >= 4:
                            dve.wait_ge(ex_mm, m - 3)
                        dve.tensor_tensor(gs[:, c, :], gel[:, c, :], at_ps[:], ALU.mult).then_inc(gs_done, 1)
                dve.wait_ge(back_ps, g + 1)
                if g:
                    dve.wait_ge(stored, 16 * g)
                dve.tensor_tensor(res[:].rearrange("p t d -> p (t d)"), kv_ps[:],
                                  x1[:, 4 * g:4 * g + 4, :].rearrange("p t d -> p (t d)"),
                                  ALU.add).then_inc(res_done, 1)

        @block.scalar
        def _(act):
            def xnT_of(c):
                act.wait_ge(xnT_ps, c + 1)
                if c >= 2:
                    act.wait_ge(v_mm, c - 1)
                act.copy(xnT[:, c % 2, :], x_ps[:]).then_inc(xnT_sb, 1)

            def hi_of(c):
                act.wait_ge(qk_mm, c + 1)
                act.copy(qk_hi[:, :, c * TC * P:(c + 1) * TC * P],
                         feat_ps[:, 2 * (c % 2):2 * (c % 2) + 2, :]).then_inc(hi_done, 1)

            def v_of(c):
                act.wait_ge(v_mm, c + 1)
                act.copy(v_all[:, c * TC:(c + 1) * TC, :],
                         mix_ps[:].rearrange("p (t d) -> p t d", d=D)).then_inc(v_done, 1)

            xnT_of(0)
            for c in range(CH):
                hi_of(c)
                if c + 1 < CH:
                    xnT_of(c + 1)
                v_of(c)

            def body(b, k, r, units, tail, norm):
                for u in range(U):
                    if units:
                        act.wait_ge(feat_mm, b * U + (u + 1))
                        act.activation(exps[:, u % RING, :], feat_ps[:, u % RING, :], ACT.Exp,
                                       bias=-1.0).then_inc(exp_done, 1)
                    if tail and u == 5:
                        act.wait_ge(feat_used, b * U)
                        act.copy(atT[:], at_ps[:]).then_inc(atT_sb, 1)
                    if norm and u == 9:
                        act.wait_ge(xn2T_ps, b - 1)
                        act.copy(xn2T_v[:, b - 2, :], at_ps[:, N:2 * N]).then_inc(xn2T_sb, 1)
                    if units and u == 12:
                        act.wait_ge(feat_used, b * U + 8)
                        act.copy(kvT[:], kv_ps[:, 0:2 * F]).then_inc(kvT_sb, 1)
                    if tail and u == 12:
                        act.wait_ge(attnT_ps, b)
                        act.copy(attnT[:], at_ps[:, 0:N]).then_inc(attnT_sb, 1)
                    if units and u == 14:
                        act.wait_ge(kvz_ps, b + 1)
                        src = kv_ps[:, 2 * F:4 * F].rearrange("p (s h l c) -> p l s h c", s=2, h=HG, l=2)
                        dst = kv_z[:].rearrange("p (s l h) c -> p l s h c", s=2, l=2)
                        for l in range(2):
                            cp = act.copy(dst[:, l, :, :, SLOT * l:SLOT * l + SLOT], src[:, l])
                        cp.then_inc(kvz_sb, 1)

            act.wait_ge(dve_set, 6)
            batches(act, body)
            act.wait_ge(route, 2)
            act.activation(lexp[:], lexp[:], ACT.Exp).then_inc(lexp_done, 1)
            act.wait_ge(ffw_in, 64)
            for g in range(NG):
                act.wait_ge(gateT_ps, g + 1)
                act.copy(gateT[:, g * GT:(g + 1) * GT], x_ps[0:E, :]
                         ).then_inc(gateT_sb, 1)
            for g in range(NG):
                for e in range(E):
                    for c in range(C):
                        m = (g * E + e) * C + c
                        act.wait_ge(hid_mm, m + 1)
                        if m >= 4:
                            act.wait_ge(gs_done, m - 3)
                        act.activation(gel[:, c, :], feat_ps[:, c, :], ACT.Gelu_apprx_tanh,
                                       bias=b1_s[:, e, c:c + 1]).then_inc(gelu_done, 1)
                act.wait_ge(ex_mm, (g + 1) * E * C)
                act.copy(yT[:], mix_ps[:]).then_inc(yT_sb, 1)

        @block.tensor
        def _(pe):
            pe.wait_ge(consts_in, 16 * CONSTS)

            def xnT_of(c):
                pe.wait_ge(ln_xn, TC * (c + 1))
                if c:
                    pe.wait_ge(xnT_sb, c)
                for j in range(TC):
                    mm = pe.transpose(x_ps[:, j * P:(j + 1) * P], xn[:, c % 2, j, :], ident_s[:])
                mm.then_inc(xnT_ps, 1)

            def qk_of(c):
                pe.wait_ge(xnT_sb, c + 1)
                if c >= 2:
                    pe.wait_ge(lo_done, c - 1)
                for s in range(2):
                    mm = pe.matmul(feat_ps[:, 2 * (c % 2) + s, :], wqkvT_s[:, s * D:(s + 1) * D], xnT[:, c % 2, :],
                                   start=True, stop=True)
                mm.then_inc(qk_mm, 1)

            def v_of(c):
                if c:
                    pe.wait_ge(v_done, c)
                for j in range(TC):
                    mm = pe.matmul(mix_ps[:, j * D:(j + 1) * D], xnT[:, c % 2, j * P:(j + 1) * P],
                                   wqkvT_s[:, 2 * D:3 * D], start=True, stop=True)
                mm.then_inc(v_mm, 1)

            xnT_of(0)
            for c in range(CH):
                qk_of(c)
                if c + 1 < CH:
                    xnT_of(c + 1)
                v_of(c)

            pe.wait_ge(proj_split, 2)
            pe.wait_ge(dve_set, 6)
            pe.wait_ge(lo_done, CH)
            pe.wait_ge(v_done, CH)

            def feature(k, u):
                bank = u % RING
                if u < 8:
                    g, j = u // 2, u % 2
                    mm = pe.matmul(feat_ps[:, bank, :], stack[:, k, g, 1, j * P:(j + 1) * P],
                                   proj_st[:, g * 512:(g + 1) * 512], start=True, stop=True)
                else:
                    for h in (2 * (u - 8), 2 * (u - 8) + 1):
                        mm = pe.matmul(feat_ps[:, bank, (h % 2) * N:(h % 2 + 1) * N],
                                       proj_st[:, h * F:(h + 1) * F], stack[:, k, h // HG, 0, :],
                                       start=True, stop=True)
                mm.then_inc(feat_mm, 1)

            def kv_round(k, u):
                g, j = u // 2, u % 2
                for h in range(HG):
                    mm = pe.matmul(kv_ps[32 * h:32 * h + 32, (g // 2) * F:(g // 2 + 1) * F],
                                   v_z[:, k, j, HG * g + h, :], feats[:, u, h * F:(h + 1) * F],
                                   start=(g % 2 == 0 and j == 0), stop=(g % 2 == 1 and j == 1))
                mm.then_inc(feat_used, 1)

            def attn_round(g):
                for h in range(HG):
                    mm = pe.matmul(at_ps[32 * h:32 * h + 32, (g // 2) * N:(g // 2 + 1) * N],
                                   kv_z[:, HG * g + h, :], feats[:, 2 * g + h // 2, (h % 2) * N:(h % 2 + 1) * N],
                                   start=(g % 2 == 0), stop=(g % 2 == 1))
                mm.then_inc(feat_used, 2)

            def body(b, k, r, units, tail, norm):
                if units:
                    pe.wait_ge(stack_in[k], r * (12 * 16) + 12 * 16)
                for u in range(U):
                    if units:
                        if not (isinstance(b, int) and b * U + u < RING):
                            pe.wait_ge(feat_done, b * U + (u + 1 - RING))
                        feature(k, u)
                    if tail and u in (1, 2, 4):
                        if not units and u == 1:
                            pe.wait_ge(feat_done, b * U)
                        attn_round((1, 2, 2, 3)[u - 1])
                    if units and u == 4:
                        pe.wait_ge(vz_done, b * 2 + 2)
                    if units and 4 <= u < 12:
                        kv_round(k, u - 4)
                    if tail and u == 7:
                        pe.wait_ge(atT_sb, b)
                        if norm:
                            pe.wait_ge(x1_done, b - 1)
                        for j in range(TPB):
                            for s in range(2):
                                mm = pe.transpose(mix_ps[:, (2 * j + s) * P:(2 * j + s + 1) * P],
                                                  atT[:, s * N + j * P:s * N + (j + 1) * P], ident_s[:])
                        mm.then_inc(atok_ps, 1)
                    if norm and u == 8:
                        pe.wait_ge(l2_xn, b * 2 - 2)
                        for j in range(TPB):
                            mm = pe.transpose(at_ps[:, N + j * P:N + (j + 1) * P], xn2[:, j, :], ident_s[:])
                        mm.then_inc(xn2T_ps, 1)
                    if tail and u == 11:
                        pe.wait_ge(attn_done, b)
                        if norm:
                            pe.wait_ge(xn2T_sb, b - 1)
                        for j in range(TPB):
                            mm = pe.transpose(at_ps[:, j * P:(j + 1) * P], attn[:, j, :], ident_s[:])
                        mm.then_inc(attnT_ps, 1)
                    if units and u == 13:
                        pe.wait_ge(kvT_sb, b + 1)
                        for s in range(2):
                            mm = pe.transpose(kv_ps[:, (2 + s) * F:(3 + s) * F], kvT[:, s * F:(s + 1) * F], ident_s[:])
                        mm.then_inc(kvz_ps, 1)
                    if tail and u == 14:
                        pe.wait_ge(attnT_sb, b)
                        for j in range(TPB):
                            mm = pe.matmul(mix_ps[:, j * D:(j + 1) * D], attnT[:, j * P:(j + 1) * P], woT_s[:],
                                           start=True, stop=True)
                        mm.then_inc(y_mm, 1)
                    if units and u == 15:
                        pe.wait_ge(kvz_sb, b + 1)
                        attn_round(0)

            batches(pe, body)
            pe.wait_ge(xn2T_sb, B)
            for t in range(T):
                mm = pe.matmul(mix_ps[:, t * E:(t + 1) * E], xn2T[:, t * P:(t + 1) * P], wr_s[:], start=True, stop=True)
                mm.then_inc(logit_mm, 1)
            pe.wait_ge(route, 12)
            for g in range(NG):
                if g:
                    pe.wait_ge(gateT_sb, g)
                for t in range(4):
                    mm = pe.transpose(x_ps[0:E, t * P:(t + 1) * P], gate[:, 4 * g + t, :], ident_s[:])
                mm.then_inc(gateT_ps, 1)
            pe.wait_ge(gateT_sb, NG)
            pe.wait_ge(ffw_in, 64)

            def up(m):
                g, e, c = m // (E * C), m // C % E, m % C
                if m >= 4:
                    pe.wait_ge(gelu_done, m - 3)
                pe.matmul(feat_ps[:, c, :], w1_s[:, e, c * P:(c + 1) * P], xn2T[:, g * GT:(g + 1) * GT],
                          start=True, stop=True).then_inc(hid_mm, 1)

            def down(m):
                g, e, c = m // (E * C), m // C % E, m % C
                if m % (E * C) == 0:
                    if g:
                        pe.wait_ge(yT_sb, g)
                    pe.matmul(mix_ps[:], b2_s[:], gateT[:, g * GT:(g + 1) * GT], start=True, stop=False)
                if c == 0:
                    if m:
                        pe.wait_ge(gs_done, m)
                    pe.matmul(at_ps[:], pick_s[:, e, :], gateT[:, g * GT:(g + 1) * GT], start=True,
                              stop=True).then_inc(wb_mm, 1)
                pe.wait_ge(gs_done, m + 1)
                pe.matmul(mix_ps[:], w2_s[:, e, c, :], gs[:, c, :], start=False,
                          stop=(m % (E * C) == E * C - 1)).then_inc(ex_mm, 1)

            M = NG * E * C
            for m in range(M + 4):
                if m < M:
                    up(m)
                if m >= 4:
                    down(m - 4)
                    if (m - 3) % (E * C) == 0:
                        g = (m - 3) // (E * C) - 1
                        pe.wait_ge(yT_sb, g + 1)
                        if g:
                            pe.wait_ge(res_done, g)
                        for t in range(4):
                            mm = pe.transpose(kv_ps[:, t * P:(t + 1) * P], yT[:, t * P:(t + 1) * P], ident_s[:])
                        mm.then_inc(back_ps, 1)


_OUT = (B, N, D)


def kernel(L0_attn_x, L0_attn_W_qkv, L0_attn_proj, L0_attn_W_out, L0_attn_b_out, L0_ffn_w_router,
           L0_ffn_w1, L0_ffn_b1, L0_ffn_w2, L0_ffn_b2):
    import numpy as np
    import concourse.bacc as bacc
    from concourse.bass_utils import run_bass_kernel_spmd

    proj = np.asarray(L0_attn_proj)
    proj3 = np.zeros((3, HG, HD, G, HG, F), proj.dtype)
    for j in range(HG):
        proj3[:, j, :, :, j, :] = proj.reshape(G, HG, HD, F)[:, j].transpose(1, 0, 2)
    pick = np.zeros((E, E, P), np.float32)
    for e in range(E):
        pick[e, e, :] = 1.0
    arrays = {
        "x": np.asarray(L0_attn_x).reshape(T * P, D),
        "wqkvT": np.asarray(L0_attn_W_qkv).T,
        "proj3": proj3.reshape(96, H * F),
        "woT": np.asarray(L0_attn_W_out).T.reshape(2, 2, HG, HD, D).transpose(0, 2, 1, 3, 4).reshape(D, D),
        "bout": np.tile(np.asarray(L0_attn_b_out).reshape(1, D), (P, 1)),
        "wr": np.asarray(L0_ffn_w_router),
        "w1": np.asarray(L0_ffn_w1),
        "b1": np.asarray(L0_ffn_b1).reshape(E, C, P).transpose(2, 0, 1),
        "w2": np.asarray(L0_ffn_w2),
        "b2": np.asarray(L0_ffn_b2),
        "ident": np.eye(P, dtype=np.float32),
        "expert_no": np.tile(np.arange(E, dtype=np.float32), (P, 1)),
        "pick": pick,
    }
    arrays = {k: np.ascontiguousarray(v) for k, v in arrays.items()}
    nc = bacc.Bacc("TRN2", target_bir_lowering=False, num_devices=1)
    args = [nc.dram_tensor(k, v.shape, mybir.dt.from_np(v.dtype), kind="ExternalInput").ap() for k, v in arrays.items()]
    out = nc.dram_tensor("out", (T * P, D), F32, kind="ExternalOutput").ap()
    build(nc, *args, out)
    r = run_bass_kernel_spmd(nc, [arrays], core_ids=[0])
    return r.results[0]["out"].reshape(B, N, D)
```

```python
import math
from contextlib import ExitStack

import concourse.bass as bass
from concourse import mybir

F32 = mybir.dt.float32
F32R = mybir.dt.float32r
U32 = mybir.dt.uint32
ALU = mybir.AluOpType
ACT = mybir.ActivationFunctionType
AX = mybir.AxisListType

P = 128
D = 128
B, N = 8, 256
T = B * N // P
TPB = N // P
H, HD, F = 16, 8, 128
G = 4
HG = H // G
KS = 97
U = 16
RING = 4
FR = 8
SLOT = 16
CH = 4
TC = T // CH
E, HID = 8, 512
C = HID // P
GT = 512
TG = GT // P
NG = T * P // GT
EPS = 1e-5
LAG = 3
UE = E * C
WARM_UP = 3
CONSTS = 6


def build(nc, x, wqkvT, proj3, woT, bout, wr, wcat, b1, b2, ident, expert_no, gates_dram, out):
    with ExitStack() as ctx:
        def sb(name, shape, dt=F32):
            return ctx.enter_context(nc.sbuf_tensor(name, shape, dt))

        def ps(name, shape):
            return ctx.enter_context(nc.psum_tensor(name, shape, F32))

        def sem(name):
            return ctx.enter_context(nc.semaphore(name))

        ident_s = sb("ident_s", [P, P])
        wqkvT_s = sb("wqkvT_s", [D, 3 * D])
        woT_s = sb("woT_s", [D, D])
        bout_s = sb("bout_s", [P, D])
        proj_st = sb("proj_st", [KS, H * F], F32R)
        wr_s = sb("wr_s", [D, E])
        w_raw = sb("w_raw", [P, 2, 2, HID])
        w_hi = sb("w_hi", [P, 2, E, HID], F32R)
        w_lo = sb("w_lo", [P, 2, E, HID], F32R)
        b1_s = sb("b1_s", [P, E, C])
        b2_s = sb("b2_s", [D, E])
        expert_no_s = sb("expert_no_s", [P, E])
        half_neg = sb("half_neg", [P, TC])
        euler = sb("euler", [P, (TG) * E])
        warm = sb("warm", [P, 1])

        x_all = sb("x_all", [P, T, D])
        stats = sb("stats", [P, T, 6])
        mv = sb("mv", [P, T, 2])
        rstd = sb("rstd", [P, T])
        qk_hi = sb("qk_hi", [D, 2, T * P], F32R)
        qk_lo = sb("qk_lo", [D, 2, T * P], F32R)
        v_all = sb("v_all", [P, T, D])
        v_z = sb("v_z", [P, 2, TPB, H, 2 * SLOT])
        stack = sb("stack", [KS, 2, G, 2, N], F32R)
        exps = sb("exps", [P, RING, 512])
        feats = sb("feats", [P, FR, 512])
        xn = feats[:, 0:2, :].rearrange("p k (j d) -> p k j d", d=D)
        proj_raw = feats[0:KS, 4:8, :].rearrange("p a n -> p (a n)")
        xnT = exps[:, 0:2, :]
        kvT = sb("kvT", [P, 2 * F])
        kv_z = sb("kv_z", [F, H, 2 * SLOT])
        atT = sb("atT", [P, 2 * N])
        rden = sb("rden", [P, TPB * H])
        attn = sb("attn", [P, TPB, D])
        attnT = sb("attnT", [D, N])
        stats2 = sb("stats2", [P, TPB, 6])
        mv2 = sb("mv2", [P, TPB, 2])
        rstd2 = sb("rstd2", [P, TPB])
        x1_cur = sb("x1_cur", [P, 2, TPB, D])
        xn2 = sb("xn2", [P, TPB, D])
        xn2T = v_all[:].rearrange("p t d -> p (t d)")
        lmax = sb("lmax", [P, T])
        lexp = sb("lexp", [P, T, E])
        lsum = sb("lsum", [P, T])
        probs = sb("probs", [P, T, E])
        top8 = sb("top8", [P, T, 8])
        topi = sb("topi", [P, T, 8], U32)
        topf = sb("topf", [P, T, 2])
        chosen = sb("chosen", [P, 2, T, E])
        gate = sb("gate", [P, T, E])
        gate_T = sb("gate_T", [E, 2, GT])
        res = sb("res", [P, TG, D])
        gel = feats[:, 0:4, :]
        acc = feats[:, 4, :]
        gated = feats[:, 6:8, :]
        gate_w = exps[:, 0:2, :]
        gel_hi = qk_hi[:, 0, :].rearrange("p (a n) -> p a n", n=GT)
        gel_lo = qk_lo[:, 0, :].rearrange("p (a n) -> p a n", n=GT)
        x_hi = qk_hi[:, 1, :].rearrange("p (g n) -> p g n", n=GT)
        x_lo = qk_lo[:, 1, :].rearrange("p (g n) -> p g n", n=GT)

        feat_ps = ps("feat_ps", [P, RING, 512])
        kv_ps = ps("kv_ps", [P, 512])
        at_ps = ps("at_ps", [P, 512])
        mix_ps = ps("mix_ps", [P, 512])
        x_ps = ps("x_ps", [P, 512])


        consts_in = sem("consts_in")
        first_in = sem("first_in")
        ones_in = sem("ones_in")
        projw_in = sem("projw_in")
        gate_in = [sem("gate_in_even"), sem("gate_in_odd")]
        w_in = [sem("w_in_even"), sem("w_in_odd")]
        x_in = [sem("x_in_0"), sem("x_in_1"), sem("x_in_rest")]
        pool_set = sem("pool_set")
        zeros_set = sem("zeros_set")
        proj_split = sem("proj_split")
        ln_stats = sem("ln_stats")
        ln_mv = sem("ln_mv")
        ln_veps = sem("ln_veps")
        ln_rstd = sem("ln_rstd")
        ln_xn = sem("ln_xn")
        xb_done = sem("xb_done")
        xnT_ps = sem("xnT_ps")
        xnT_sb = sem("xnT_sb")
        qk_mm = sem("qk_mm")
        v_mm = sem("v_mm")
        hi_done = sem("hi_done")
        lo_done = sem("lo_done")
        v_done = sem("v_done")
        feat_mm = sem("feat_mm")
        exp_done = sem("exp_done")
        feat_done = sem("feat_done")
        feat_used = sem("feat_used")
        vz_done = sem("vz_done")
        kvT_sb = sem("kvT_sb")
        kvz_ps = sem("kvz_ps")
        kvz_sb = sem("kvz_sb")
        atT_sb = sem("atT_sb")
        atok_ps = sem("atok_ps")
        den_done = sem("den_done")
        rden_done = sem("rden_done")
        attn_done = sem("attn_done")
        attnT_ps = sem("attnT_ps")
        attnT_sb = sem("attnT_sb")
        y_mm = sem("y_mm")
        x1_done = sem("x1_done")
        x1_kept = sem("x1_kept")
        l2_stats = sem("l2_stats")
        l2_mv = sem("l2_mv")
        l2_veps = sem("l2_veps")
        l2_rstd = sem("l2_rstd")
        l2_xn = sem("l2_xn")
        xn2T_ps = sem("xn2T_ps")
        xn2T_sb = sem("xn2T_sb")
        logit_mm = sem("logit_mm")
        route = sem("route")
        lexp_done = sem("lexp_done")
        whi_done = sem("whi_done")
        wlo_done = sem("wlo_done")
        xhi_done = sem("xhi_done")
        xlo_done = sem("xlo_done")
        gates_done = sem("gates_done")
        shifted = sem("shifted")
        gateT_ps = sem("gateT_ps")
        gateT_sb = sem("gateT_sb")
        gate_out = sem("gate_out")
        hid_mm = sem("hid_mm")
        gelu_done = sem("gelu_done")
        ghi_act = sem("ghi_act")
        ghi_dve = sem("ghi_dve")
        glo_done = sem("glo_done")
        down_mm = sem("down_mm")
        gated_done = sem("gated_done")
        acc_done = sem("acc_done")
        back_ps = sem("back_ps")
        res_done = sem("res_done")
        stored = sem("stored")
        dve_met = sem("dve_met")
        pool_met = sem("pool_met")
        sp_met = sem("sp_met")
        stack_in = [sem("stack_in_even"), sem("stack_in_odd")]
        stack_first = [sem(f"stack_first_{g}") for g in range(G)]

        logits_at = ((0, T - TG, kv_ps), (T - TG, T, at_ps))

        def is_first(b):
            return isinstance(b, int) and b == 0

        def batches(eng, body):
            body(0, 0, 0, True, False, False)
            body(1, 1, 0, True, True, False)
            with eng.Fori(0, B // 2 - 1) as i:
                body(i * 2 + 2, 0, i + 1, True, True, True)
                body(i * 2 + 3, 1, i + 1, True, True, True)

        GATES_AT = {2: 0, 18: 1, 22: 2, 28: 3}

        def xnT_bank(c):
            return x_ps if c % 2 == 0 else kv_ps

        def gate_bank(q):
            return kv_ps if q == 0 else at_ps

        def groups(eng, body):
            body(0, True, False)
            body(1, True, True)
            with eng.Fori(2, NG) as g:
                body(g, True, True)
            body(NG, False, True)

        x1_v = x_all[:].rearrange("p (b j) d -> p b (j d)", j=TPB)
        xn2T_v = xn2T.rearrange("p (b n) -> p b n", n=N)

        block = ctx.enter_context(nc.Block())

        @block.sync
        def _(sp):
            xt = x.rearrange("(t p) d -> p t d", p=P)
            sp.dma_start(x_all[:, 0:TC, :], xt[:, 0:TC, :]).then_inc(x_in[0], 16)
            sp.dma_start(ident_s[:], ident).then_inc(first_in, 16)
            sp.dma_start(wqkvT_s[:], wqkvT).then_inc(first_in, 16)
            sp.dma_start(x_all[:, TC:2 * TC, :], xt[:, TC:2 * TC, :]).then_inc(x_in[1], 16)
            sp.dma_start(proj_raw, proj3).then_inc(projw_in, 16)
            sp.dma_start(x_all[:, 2 * TC:T, :], xt[:, 2 * TC:T, :]).then_inc(x_in[2], 16)
            for k in range(2):
                sp.dma_start(w_raw[:, k, :, :], wcat[k]).then_inc(w_in[k], 16)

            hi_v = qk_hi[:].bitcast(F32).rearrange("p s (b n) -> p s b n", n=N)
            lo_v = qk_lo[:].bitcast(F32).rearrange("p s (b n) -> p s b n", n=N)
            st = stack[:].bitcast(F32)

            def stack_batch(b, k, hi_rows, lo_rows):
                for g in range(G):
                    there = stack_first[g] if is_first(b) else stack_in[k]
                    rows = slice(32 * g, 32 * g + 32)
                    for at, src in ((0, hi_rows), (32, lo_rows), (64, hi_rows)):
                        sp.dma_start(st[at:at + 32, k, g, :, :], src[rows]).then_inc(there, 16)

            sp.dma_start(woT_s[:], woT).then_inc(consts_in, 16)
            sp.dma_start(bout_s[:], bout).then_inc(consts_in, 16)
            sp.dma_start(wr_s[:], wr).then_inc(consts_in, 16)
            sp.dma_start(expert_no_s[:], expert_no).then_inc(consts_in, 16)
            sp.dma_start(b1_s[:], b1).then_inc(consts_in, 16)
            sp.dma_start(b2_s[:], b2).then_inc(consts_in, 16)

            sp.wait_ge(proj_split, 1)
            for k in range(2):
                sp.dma_start(st[96:97, k].rearrange("p g s n -> p (g s n)"),
                             proj_st[96:97, :].bitcast(F32)).then_inc(ones_in, 16)
            sp.wait_ge(hi_done, 1)
            sp.wait_ge(lo_done, 1)
            for b in range(2):
                stack_batch(b, b, hi_v[:, :, b, :], lo_v[:, :, b, :])
            wcat_v = wcat.rearrange("(i k) p w n -> i k p w n", k=2)
            hi_k = qk_hi[:].bitcast(F32).rearrange("p s (i k n) -> p s i k n", n=N, k=2)
            lo_k = qk_lo[:].bitcast(F32).rearrange("p s (i k n) -> p s i k n", n=N, k=2)
            with sp.Fori(1, B // 2) as i:
                for k in range(2):
                    sp.wait_ge(feat_mm, i * (2 * U) + (k - 1) * U)
                    sp.sem_inc(sp_met)
                    sp.wait_ge(hi_done, i + 1)
                    sp.sem_inc(sp_met)
                    sp.wait_ge(lo_done, i + 1)
                    sp.sem_inc(sp_met)
                    stack_batch(i, k, hi_k[:, :, i, k, :], lo_k[:, :, i, k, :])
                    sp.wait_ge(wlo_done, i * 2 + (k - 1))
                    sp.sem_inc(sp_met)
                    sp.dma_start(w_raw[:, k, :, :], wcat_v[i, k]).then_inc(w_in[k], 16)
            ot = out.rearrange("(g t p) d -> g p t d", p=P, t=TG)
            gates_v = gates_dram.rearrange("e (g n) -> e g n", n=GT)

            def gates_out(g):
                sp.wait_ge(gateT_sb, g + 1)
                if g:
                    sp.wait_ge(gate_out, 16 * g)
                sp.dma_start(gates_v[:, g, :], gate_T[:, g % 2, :]).then_inc(gate_out, 16)

            def body(g, units, tail):
                if is_first(g):
                    gates_out(0)
                if units:
                    sp.wait_ge(gate_out, g * 16 + 16)
                    sp.sem_inc(sp_met)
                for e in range(E if units else 4):
                    if units:
                        if not (isinstance(g, int) and g == 0 and e < 2):
                            sp.wait_ge(gated_done, g * E + (e - 1))
                            sp.sem_inc(sp_met)
                        sp.dma_start(gate_w[:, e % 2, :], gates_v[e:e + 1, g, :].to_broadcast((P, GT))
                                     ).then_inc(gate_in[e % 2], 16)
                    if is_first(g) and e >= 5:
                        gates_out(e - 4)
                    if tail and e == 3:
                        sp.wait_ge(res_done, g)
                        sp.sem_inc(sp_met)
                        sp.dma_start(ot[g - 1], res[:]).then_inc(stored, 16)

            groups(sp, body)
            sp.wait_ge(stored, 16 * NG)

        @block.gpsimd
        def _(pool):
            pool.memset(half_neg[:], -0.5).then_inc(pool_set, 1)
            pool.memset(euler[:], math.e).then_inc(pool_set, 1)

            for c in range(CH):
                ts = slice(c * TC, (c + 1) * TC)
                pool.wait_ge(ln_mv, TC * (c + 1))
                pool.tensor_scalar(rstd[:, ts], mv[:, ts, 1], EPS, None, ALU.add).then_inc(ln_veps, 1)
                pool.wait_ge(ln_veps, c + 1)
                pool.wait_ge(pool_set, 1)
                pool.tensor_tensor(rstd[:, ts], rstd[:, ts], half_neg[:], ALU.pow).then_inc(ln_rstd, 1)
            pool.memset(v_z[:], 0.0).then_inc(pool_set, 1)
            pool.memset(kv_z[:], 0.0).then_inc(pool_set, 1)
            pool.wait_ge(pool_set, 3)
            ones_at = v_z[:].rearrange("p k j (s l h) c -> p l (k j s) h c", s=2, l=2)
            for l in range(2):
                pool.memset(ones_at[:, l, :, :, SLOT * l + HD], 1.0).then_inc(pool_set, 1)
            v_src = v_all[:].rearrange("p (b j) (s l h d) -> p b l (j s) h d", j=TPB, s=2, l=2, h=HG)

            def body(b, k, r, units, tail, norm):
                if units:
                    pool.wait_ge(v_done, r + 1)
                    pool.sem_inc(pool_met)
                    if not (isinstance(b, int) and b < 2):
                        pool.wait_ge(feat_used, b * U - (2 * U - 8))
                        pool.sem_inc(pool_met)
                    for l in range(2):
                        dst = v_z[:, k, :, :, :].rearrange("p j (s l h) c -> p l (j s) h c", s=2, l=2)
                        pool.tensor_copy(dst[:, l, :, :, SLOT * l:SLOT * l + HD], v_src[:, b, l]).then_inc(vz_done, 1)
                if norm:
                    pool.wait_ge(x1_done, b - 1)
                    pool.sem_inc(pool_met)
                    pool.wait_ge(l2_mv, b * 2 - 2)
                    pool.sem_inc(pool_met)
                    pool.tensor_scalar(rstd2[:], mv2[:, :, 1], EPS, None, ALU.add).then_inc(l2_veps, 1)
                    pool.wait_ge(l2_veps, b - 1)
                    pool.tensor_tensor(rstd2[:], rstd2[:], half_neg[:, 0:TPB], ALU.pow).then_inc(l2_rstd, 1)
                    pool.wait_ge(l2_rstd, b - 1)
                    pool.sem_inc(pool_met)
                    for j in range(TPB):
                        pool.tensor_scalar(xn2[:, j, :], x1_cur[:, k, j, :], mv2[:, j, 0:1], rstd2[:, j:j + 1],
                                           ALU.subtract, ALU.mult).then_inc(l2_xn, 1)
                    pool.tensor_copy(x1_v[:, b - 2, :], x1_cur[:, k].rearrange("p j d -> p (j d)")).then_inc(x1_kept, 1)
                if is_first(b):
                    pool.wait_ge(consts_in, 16 * CONSTS)
                    pool.wait_ge(ln_xn, T)
                    pool.tensor_tensor(x_all[:], x_all[:],
                                       bout_s[:].rearrange("p (o d) -> p o d", o=1).to_broadcast((P, T, D)),
                                       ALU.add).then_inc(xb_done, 1)
                if units:
                    pool.wait_ge(whi_done, b * 2 + 2)
                    pool.tensor_tensor(w_lo[:, :, b, :], w_raw[:, k, :, :], w_hi[:, :, b, :].bitcast(F32),
                                       ALU.subtract).then_inc(wlo_done, 1)

            batches(pool, body)

            def x_lo_of(g):
                pool.wait_ge(xhi_done, g + 1)
                pool.tensor_tensor(x_lo[:, g, :], xn2T[:, g * GT:(g + 1) * GT], x_hi[:, g, :].bitcast(F32),
                                   ALU.subtract).then_inc(xlo_done, 1)

            x_lo_of(0)
            body(B, 0, B // 2, False, True, True)
            body(B + 1, 1, B // 2, False, False, True)
            x_lo_of(1)
            x_lo_of(2)

            def sum_experts(g, n_experts):
                for e in range(1, n_experts):
                    n = 7 * g + (e - 1)
                    if is_first(g) and e == 3:
                        t0 = logits_at[1][0]
                        last = lexp[:, t0:T, :].rearrange("p t e -> p (t e)")
                        pool.wait_ge(shifted, 2)
                        pool.tensor_tensor(last, euler[:], last, ALU.pow).then_inc(lexp_done, 1)
                        x_lo_of(3)
                    pool.wait_ge(gated_done, g * E + (e + 1))
                    if not (isinstance(g, int) and g == 0 and e == 1):
                        pool.wait_ge(acc_done, n)
                    pool.tensor_tensor(acc, acc, gated[:, e % 2, :], ALU.add).then_inc(acc_done, 1)

            sum_experts(0, E)
            with pool.Fori(1, NG - 1) as g:
                sum_experts(g, E)
            sum_experts(NG - 1, E - 2)

        @block.vector
        def _(dve):
            def stats_of(c):
                for t in range(c * TC, (c + 1) * TC):
                    dve.bn_stats(stats[:, t, :], x_all[:, t, :]).then_inc(ln_stats, 1)
                dve.wait_ge(ln_stats, (c + 1) * TC)
                for t in range(c * TC, (c + 1) * TC):
                    dve.bn_aggr(mv[:, t, :], stats[:, t, :]).then_inc(ln_mv, 1)

            def norm_of(c):
                dve.wait_ge(ln_rstd, c + 1)
                if c >= 2:
                    dve.wait_ge(xnT_ps, c - 1)
                for j in range(TC):
                    t = c * TC + j
                    dve.tensor_scalar(xn[:, c % 2, j, :], x_all[:, t, :], mv[:, t, 0:1], rstd[:, t:t + 1],
                                      ALU.subtract, ALU.mult).then_inc(ln_xn, 1)

            def lo_of(c):
                dve.wait_ge(hi_done, c + 1)
                cs = slice(c * TC * P, (c + 1) * TC * P)
                dve.tensor_tensor(qk_lo[:, :, cs], feat_ps[:, 2 * (c % 2):2 * (c % 2) + 2, :],
                                  qk_hi[:, :, cs].bitcast(F32), ALU.subtract).then_inc(lo_done, 1)

            dve.memset(atT[:], 0.0).then_inc(zeros_set, 1)
            dve.wait_ge(x_in[0], 16)
            stats_of(0)
            dve.wait_ge(x_in[1], 16)
            stats_of(1)
            norm_of(0)
            dve.wait_ge(x_in[2], 16)
            stats_of(2)
            norm_of(1)
            stats_of(3)
            norm_of(2)
            lo_of(0)
            norm_of(3)
            lo_of(1)
            dve.wait_ge(proj_split, 1)
            dve.tensor_tensor(proj_st[64:96, :], proj_raw[64:96, :], proj_st[64:96, :].bitcast(F32),
                              ALU.subtract).then_inc(proj_split, 1)
            lo_of(2)
            lo_of(3)

            by_head = mix_ps[:].rearrange("p (t c) -> p t c", c=SLOT)

            def l2_stats_of(b, k):
                dve.wait_ge(x1_done, b + 1)
                dve.sem_inc(dve_met)
                for j in range(TPB):
                    dve.bn_stats(stats2[:, j, :], x1_cur[:, k, j, :]).then_inc(l2_stats, 1)

            def l2_mv_of(b):
                dve.wait_ge(l2_stats, b * 2 + 2)
                dve.sem_inc(dve_met)
                for j in range(TPB):
                    dve.bn_aggr(mv2[:, j, :], stats2[:, j, :]).then_inc(l2_mv, 1)

            def den_of(b):
                dve.wait_ge(atok_ps, b + 1)
                dve.tensor_scalar(rden[:], by_head[:, :, HD], 1e-8, None, ALU.add).then_inc(den_done, 1)

            def rden_of(b):
                dve.wait_ge(den_done, b + 1)
                dve.reciprocal(rden[:], rden[:]).then_inc(rden_done, 1)

            def attn_of(b):
                dve.wait_ge(rden_done, b + 1)
                dve.tensor_tensor(attn[:].rearrange("p j (h d) -> p (j h) d", d=HD), by_head[:, :, 0:HD],
                                  rden[:].rearrange("p (t o) -> p t o", o=1).to_broadcast((P, TPB * H, HD)),
                                  ALU.mult).then_inc(attn_done, 1)

            def x1_of(b, k):
                dve.wait_ge(y_mm, b + 1)
                dve.tensor_tensor(x1_cur[:, k].rearrange("p j d -> p (j d)"), mix_ps[:, 0:TPB * D], x1_v[:, b, :],
                                  ALU.add).then_inc(x1_done, 1)

            def body(b, k, r, units, tail, norm):
                for u in range(U):
                    dve.wait_ge(exp_done, b * U + (u + 1))
                    if not (isinstance(b, int) and b * U + u < FR):
                        dve.wait_ge(feat_used, b * U + (u + 1 - FR))
                    dve.scalar_tensor_tensor(out=feats[:, u % FR, :], in0=exps[:, u % RING, :], scalar=1.0,
                                             in1=feat_ps[:, u % RING, :], op0=ALU.min, op1=ALU.max
                                             ).then_inc(feat_done, 1)
                    if norm and u == 0:
                        l2_stats_of(b - 2, k)
                    if norm and u == 1:
                        l2_mv_of(b - 2)
                    if tail and u == 6:
                        den_of(b - 1)
                    if tail and u == 7:
                        rden_of(b - 1)
                    if tail and u == 8:
                        attn_of(b - 1)
                    if tail and u == 15:
                        if isinstance(b, int):
                            dve.wait_ge(xb_done, 1)
                        x1_of(b - 1, 1 - k)

            batches(dve, body)

            l2_stats_of(B - 2, 0)
            l2_mv_of(B - 2)

            step = 0

            def link(ins):
                nonlocal step
                step += 1
                ins.then_inc(route, 1)
                dve.wait_ge(route, step)

            def over_experts(t, n):
                return t.rearrange("p (t o) -> p t o", o=1).to_broadcast((P, n, E))

            def shifted_of(r):
                t0, t1, bank = logits_at[r]
                lg = bank[:, 0:(t1 - t0) * E].rearrange("p (t e) -> p t e", e=E)
                dve.wait_ge(logit_mm, t1)
                link(dve.tensor_reduce(lmax[:, t0:t1], lg, AX.X, ALU.max))
                dve.tensor_tensor(lexp[:, t0:t1, :], lg, over_experts(lmax[:, t0:t1], t1 - t0),
                                  ALU.subtract).then_inc(shifted, 1)

            def probs_of(r):
                t0, t1, _ = logits_at[r]
                dve.wait_ge(lexp_done, r + 1)
                link(dve.tensor_reduce(lsum[:, t0:t1], lexp[:, t0:t1, :], AX.X, ALU.add))
                link(dve.reciprocal(lsum[:, t0:t1], lsum[:, t0:t1]))
                link(dve.tensor_tensor(probs[:, t0:t1, :], lexp[:, t0:t1, :],
                                       over_experts(lsum[:, t0:t1], t1 - t0), ALU.mult))

            def largest_of(t0, t1):
                for t in range(t0, t1):
                    ins = dve.max(top8[:, t, :], probs[:, t, :])
                link(ins)
                for t in range(t0, t1):
                    ins = dve.max_index(topi[:, t, :], top8[:, t, :], probs[:, t, :])
                link(ins)
                link(dve.tensor_copy(topf[:, t0:t1, :], topi[:, t0:t1, 0:2]))

            def gates_of(t0, t1):
                en = expert_no_s[:].rearrange("p (o e) -> p o e", o=1).to_broadcast((P, t1 - t0, E))
                for c in range(2):
                    link(dve.tensor_tensor(chosen[:, c, t0:t1, :], en,
                                           topf[:, t0:t1, c:c + 1].to_broadcast((P, t1 - t0, E)), ALU.is_equal))
                link(dve.tensor_tensor(chosen[:, 0, t0:t1, :], chosen[:, 0, t0:t1, :], chosen[:, 1, t0:t1, :],
                                       ALU.add))
                dve.tensor_tensor(gate[:, t0:t1, :], probs[:, t0:t1, :], chosen[:, 0, t0:t1, :],
                                  ALU.mult).then_inc(gates_done, 1)

            shifted_of(0)
            probs_of(0)
            largest_of(0, TG)
            gates_of(0, TG)
            den_of(B - 1)
            rden_of(B - 1)
            attn_of(B - 1)

            x1_g = x_all[:].rearrange("p (g t) d -> p g (t d)", t=TG)

            def body(g, units, tail):
                for u in range(UE):
                    e, c = u // C, u % C
                    if is_first(g) and u == 4:
                        x1_of(B - 1, 1)
                    if is_first(g) and u == 5:
                        l2_stats_of(B - 1, 1)
                    if is_first(g) and u == 6:
                        l2_mv_of(B - 1)
                    if is_first(g) and u == 10:
                        largest_of(TG, T - TG)
                    if is_first(g) and u == 13:
                        gates_of(TG, T - TG)
                    if is_first(g) and u == 16:
                        shifted_of(1)
                    if is_first(g) and u == 22:
                        probs_of(1)
                    if is_first(g) and u == 24:
                        largest_of(T - TG, T)
                    if is_first(g) and u == 26:
                        gates_of(T - TG, T)
                    if units and c % 2 == 1:
                        dve.wait_ge(gelu_done, g * UE + (u + 1))
                        if not (isinstance(g, int) and g == 0 and u < 4):
                            dve.wait_ge(down_mm, g * UE + (u - 3))
                        dve.tensor_copy(gel_hi[:, c, :], gel[:, c, :]).then_inc(ghi_dve, 1)
                        dve.wait_ge(ghi_act, g * (UE // 2) + (u // 2 + 1))
                        dve.tensor_tensor(gel_lo[:, c - 1, :], gel[:, c - 1, :], gel_hi[:, c - 1, :].bitcast(F32),
                                          ALU.subtract).then_inc(glo_done, 1)
                        dve.wait_ge(ghi_dve, g * (UE // 2) + (u // 2 + 1))
                        dve.tensor_tensor(gel_lo[:, c, :], gel[:, c, :], gel_hi[:, c, :].bitcast(F32),
                                          ALU.subtract).then_inc(glo_done, 1)
                    if u % C == 3 and (units or u == 3) and not (u == 3 and not tail):
                        q = (u - 7) // C
                        ee, n = q % E, g * E + q
                        dve.wait_ge(down_mm, g * UE + (C * q + C))
                        dve.wait_ge(gate_in[ee % 2], g * (16 * E // 2) + 16 * (q // 2 + 1))
                        if ee == 0:
                            if tail:
                                dve.wait_ge(back_ps, g)
                        elif not (isinstance(g, int) and g == 0 and ee < 3):
                            dve.wait_ge(acc_done, g * 7 + {1: 0, 2: -1, 7: -2}.get(ee, ee - 2))
                        dve.scalar_tensor_tensor(out=acc if ee == 0 else gated[:, ee % 2, :],
                                                 in0=(x_ps, mix_ps)[ee % 2][:], scalar=b2_s[:, ee:ee + 1],
                                                 in1=gate_w[:, ee % 2, :], op0=ALU.add, op1=ALU.mult
                                                 ).then_inc(gated_done, 1)
                    if tail and u == 9:
                        dve.wait_ge(back_ps, g)
                        if isinstance(g, int) and g == 1:
                            dve.wait_ge(x1_kept, B)
                        else:
                            dve.wait_ge(stored, g * 16 - 16)
                        dve.tensor_tensor(res[:].rearrange("p t d -> p (t d)"), kv_ps[:], x1_g[:, g - 1, :],
                                          ALU.add).then_inc(res_done, 1)

            groups(dve, body)

        @block.scalar
        def _(act):
            def xnT_of(c):
                act.wait_ge(xnT_ps, c + 1)
                if c >= 2:
                    act.wait_ge(v_mm, c - 1)
                act.copy(xnT[:, c % 2, :], xnT_bank(c)[:]).then_inc(xnT_sb, 1)

            def hi_of(c):
                act.wait_ge(qk_mm, c + 1)
                act.copy(qk_hi[:, :, c * TC * P:(c + 1) * TC * P],
                         feat_ps[:, 2 * (c % 2):2 * (c % 2) + 2, :]).then_inc(hi_done, 1)

            def v_of(c):
                act.wait_ge(v_mm, c + 1)
                act.copy(v_all[:, c * TC:(c + 1) * TC, :],
                         mix_ps[:].rearrange("p (t d) -> p t d", d=D)).then_inc(v_done, 1)

            xnT_of(0)
            act.wait_ge(projw_in, 16)
            act.copy(proj_st[:], proj_raw).then_inc(proj_split, 1)
            hi_of(0)
            xnT_of(1)
            v_of(0)
            for c in range(1, CH):
                if c + 1 < CH:
                    xnT_of(c + 1)
                hi_of(c)
                if c + 1 < CH:
                    v_of(c)

            def atT_of(b):
                act.wait_ge(feat_used, b * U + U)
                act.copy(atT[:], at_ps[:]).then_inc(atT_sb, 1)

            def attnT_of(b):
                act.wait_ge(attnT_ps, b + 1)
                act.copy(attnT[:], at_ps[:, 0:N]).then_inc(attnT_sb, 1)

            def xn2T_of(b):
                act.wait_ge(xn2T_ps, b + 1)
                act.copy(xn2T_v[:, b, :], at_ps[:, N:2 * N]).then_inc(xn2T_sb, 1)

            def body(b, k, r, units, tail, norm):
                for u in range(U):
                    if units:
                        act.wait_ge(feat_mm, b * U + (u + 1))
                        act.activation(exps[:, u % RING, :], feat_ps[:, u % RING, :], ACT.Exp,
                                       bias=-1.0).then_inc(exp_done, 1)
                    if is_first(b) and u == 1:
                        v_of(CH - 1)
                    if tail and u == 5:
                        atT_of(b - 1)
                    if norm and u == 10:
                        xn2T_of(b - 2)
                    if units and u in (2, 3):
                        w = u - 2
                        act.wait_ge(w_in[k], r * 16 + 16)
                        act.copy(w_hi[:, w, b, :], w_raw[:, k, w, :]).then_inc(whi_done, 1)
                    if units and u == 11:
                        act.wait_ge(feat_used, b * U + 8)
                        act.copy(kvT[:], kv_ps[:, 0:2 * F]).then_inc(kvT_sb, 1)
                    if tail and u == 12:
                        attnT_of(b - 1)
                    if units and u == 13:
                        act.wait_ge(kvz_ps, b + 1)
                        src = kv_ps[:, 2 * F:4 * F].rearrange("p (s h l c) -> p l s h c", s=2, h=HG, l=2)
                        dst = kv_z[:].rearrange("p (s l h) c -> p l s h c", s=2, l=2)
                        for l in range(2):
                            cp = act.copy(dst[:, l, :, :, SLOT * l:SLOT * l + SLOT], src[:, l])
                        cp.then_inc(kvz_sb, 1)

            act.wait_ge(pool_set, 4)
            batches(act, body)

            def x_hi_of(g):
                act.wait_ge(xn2T_sb, 2 * g + 2)
                act.copy(x_hi[:, g, :], xn2T[:, g * GT:(g + 1) * GT]).then_inc(xhi_done, 1)

            x_hi_of(0)
            t1 = logits_at[0][1]
            act.wait_ge(shifted, 1)
            act.activation(lexp[:, 0:t1, :], lexp[:, 0:t1, :], ACT.Exp).then_inc(lexp_done, 1)
            act.wait_ge(pool_set, 1)
            act.activation(warm[:], half_neg[:, 0:1], ACT.Gelu_apprx_tanh)
            atT_of(B - 1)

            def body(g, units, tail):
                for u in range(UE if units else 0):
                    e, c = u // C, u % C
                    act.wait_ge(hid_mm, g * UE + (u + 1))
                    if not (isinstance(g, int) and g == 0 and u < 4):
                        act.wait_ge(glo_done, g * UE + (u - 3))
                    act.activation(gel[:, c, :], feat_ps[:, c, :], ACT.Gelu_apprx_tanh,
                                   bias=b1_s[:, e, c:c + 1]).then_inc(gelu_done, 1)
                    if is_first(g) and u == 2:
                        xn2T_of(B - 2)
                    if is_first(g) and u == 4:
                        attnT_of(B - 1)
                    if is_first(g) and u == 11:
                        xn2T_of(B - 1)
                    if is_first(g) and u in (6, 8, 14):
                        x_hi_of({6: 1, 8: 2, 14: 3}[u])
                    if c % 2 == 1:
                        act.wait_ge(gelu_done, g * UE + u)
                        if not (isinstance(g, int) and g == 0 and u < 5):
                            act.wait_ge(down_mm, g * UE + (u - 4))
                        act.copy(gel_hi[:, c - 1, :], gel[:, c - 1, :]).then_inc(ghi_act, 1)
                    if is_first(g) and u - 1 in GATES_AT:
                        q = GATES_AT[u - 1]
                        act.wait_ge(gateT_ps, q + 1)
                        if q >= 2:
                            act.wait_ge(gate_out, 16 * (q - 1))
                        act.copy(gate_T[:, q % 2, :], gate_bank(q)[0:E, :]).then_inc(gateT_sb, 1)

            groups(act, body)

        @block.tensor
        def _(pe):
            pe.wait_ge(zeros_set, 1)
            for _ in range(WARM_UP):
                pe.matmul(mix_ps[:], atT[:, 0:P], atT[:], start=True, stop=True)
            pe.wait_ge(first_in, 32)

            def xnT_of(c):
                pe.wait_ge(ln_xn, TC * (c + 1))
                if c >= 2:
                    pe.wait_ge(xnT_sb, c - 1)
                for j in range(TC):
                    mm = pe.transpose(xnT_bank(c)[:, j * P:(j + 1) * P], xn[:, c % 2, j, :], ident_s[:])
                mm.then_inc(xnT_ps, 1)

            def qk_of(c):
                pe.wait_ge(xnT_sb, c + 1)
                if c >= 2:
                    pe.wait_ge(lo_done, c - 1)
                for s in range(2):
                    mm = pe.matmul(feat_ps[:, 2 * (c % 2) + s, :], wqkvT_s[:, s * D:(s + 1) * D], xnT[:, c % 2, :],
                                   start=True, stop=True)
                mm.then_inc(qk_mm, 1)

            def v_of(c):
                if c:
                    pe.wait_ge(v_done, c)
                for j in range(TC):
                    mm = pe.matmul(mix_ps[:, j * D:(j + 1) * D], xnT[:, c % 2, j * P:(j + 1) * P],
                                   wqkvT_s[:, 2 * D:3 * D], start=True, stop=True)
                mm.then_inc(v_mm, 1)

            xnT_of(0)
            qk_of(0)
            xnT_of(1)
            v_of(0)
            for c in range(1, CH):
                if c + 1 < CH:
                    xnT_of(c + 1)
                qk_of(c)
                if c + 1 < CH:
                    v_of(c)

            pe.wait_ge(proj_split, 2)
            pe.wait_ge(ones_in, 2 * 16)
            pe.wait_ge(lo_done, CH - 1)

            def feature(k, u):
                bank = u % RING
                if u < 8:
                    g, j = u // 2, u % 2
                    mm = pe.matmul(feat_ps[:, bank, :], stack[:, k, g, 1, j * P:(j + 1) * P],
                                   proj_st[:, g * 512:(g + 1) * 512], start=True, stop=True)
                else:
                    for h in (2 * (u - 8), 2 * (u - 8) + 1):
                        mm = pe.matmul(feat_ps[:, bank, (h % 2) * N:(h % 2 + 1) * N],
                                       proj_st[:, h * F:(h + 1) * F], stack[:, k, h // HG, 0, :],
                                       start=True, stop=True)
                mm.then_inc(feat_mm, 1)

            def kv_round(k, u):
                g, j = u // 2, u % 2
                for h in range(HG):
                    mm = pe.matmul(kv_ps[32 * h:32 * h + 32, (g // 2) * F:(g // 2 + 1) * F],
                                   v_z[:, k, j, HG * g + h, :], feats[:, u, h * F:(h + 1) * F],
                                   start=(g % 2 == 0 and j == 0), stop=(g % 2 == 1 and j == 1))
                mm.then_inc(feat_used, 1)

            def attn_round(g):
                for h in range(HG):
                    mm = pe.matmul(at_ps[32 * h:32 * h + 32, (g // 2) * N:(g // 2 + 1) * N],
                                   kv_z[:, HG * g + h, :], feats[:, 2 * g + h // 2, (h % 2) * N:(h % 2 + 1) * N],
                                   start=(g % 2 == 0), stop=(g % 2 == 1))
                mm.then_inc(feat_used, 2)

            def atok_of(b):
                pe.wait_ge(atT_sb, b + 1)
                for j in range(TPB):
                    for s in range(2):
                        mm = pe.transpose(mix_ps[:, (2 * j + s) * P:(2 * j + s + 1) * P],
                                          atT[:, s * N + j * P:s * N + (j + 1) * P], ident_s[:])
                mm.then_inc(atok_ps, 1)

            def attnT_of(b):
                pe.wait_ge(attn_done, b + 1)
                for j in range(TPB):
                    mm = pe.transpose(at_ps[:, j * P:(j + 1) * P], attn[:, j, :], ident_s[:])
                mm.then_inc(attnT_ps, 1)

            def y_of(b):
                pe.wait_ge(attnT_sb, b + 1)
                for j in range(TPB):
                    mm = pe.matmul(mix_ps[:, j * D:(j + 1) * D], attnT[:, j * P:(j + 1) * P], woT_s[:],
                                   start=True, stop=True)
                mm.then_inc(y_mm, 1)

            def xn2T_of(b):
                pe.wait_ge(l2_xn, b * 2 + 2)
                for j in range(TPB):
                    mm = pe.transpose(at_ps[:, N + j * P:N + (j + 1) * P], xn2[:, j, :], ident_s[:])
                mm.then_inc(xn2T_ps, 1)

            def body(b, k, r, units, tail, norm):
                if not is_first(b):
                    pe.wait_ge(stack_in[k], r * (12 * 16) + 12 * 16 * k)
                for u in range(U):
                    if is_first(b) and u == 2:
                        pe.wait_ge(lo_done, CH)
                    if is_first(b) and u < 8 and u % 2 == 0:
                        pe.wait_ge(stack_first[u // 2], 3 * 16)
                    if units:
                        if not (isinstance(b, int) and b * U + u < RING):
                            pe.wait_ge(feat_done, b * U + (u + 1 - RING))
                        feature(k, u)
                    if is_first(b) and u == 0:
                        v_of(CH - 1)
                    if tail and u in (2, 3, 4):
                        attn_round(u - 1)
                    if units and u == 4:
                        pe.wait_ge(vz_done, b * 2 + 2)
                    if units and 4 <= u < 12:
                        kv_round(k, u - 4)
                    if tail and u == 7:
                        if norm:
                            pe.wait_ge(x1_done, b - 1)
                        atok_of(b - 1)
                    if norm and u == 9:
                        xn2T_of(b - 2)
                    if tail and u == 11:
                        if norm:
                            pe.wait_ge(xn2T_sb, b - 1)
                        attnT_of(b - 1)
                    if units and u == 13:
                        pe.wait_ge(kvT_sb, b + 1)
                        for s in range(2):
                            mm = pe.transpose(kv_ps[:, (2 + s) * F:(3 + s) * F], kvT[:, s * F:(s + 1) * F], ident_s[:])
                        mm.then_inc(kvz_ps, 1)
                    if tail and u == 14:
                        if isinstance(b, int):
                            pe.wait_ge(consts_in, 16 * CONSTS)
                        y_of(b - 1)
                    if units and u == 15:
                        pe.wait_ge(kvz_sb, b + 1)
                        attn_round(0)

            batches(pe, body)

            def logits_of(r):
                t0, t1, bank = logits_at[r]
                pe.wait_ge(xn2T_sb, t1 // TPB)
                for t in range(t0, t1):
                    mm = pe.matmul(bank[:, (t - t0) * E:(t - t0 + 1) * E], xn2T[:, t * P:(t + 1) * P], wr_s[:],
                                   start=True, stop=True)
                    mm.then_inc(logit_mm, 1)

            logits_of(0)
            pe.wait_ge(feat_done, B * U)
            for g in (1, 2, 3):
                attn_round(g)
            pe.wait_ge(wlo_done, E)

            def up(g, u):
                e, c = u // C, u % C
                lhs = slice(c * P, (c + 1) * P)
                for i, (w, xs) in enumerate(((w_hi, x_hi), (w_hi, x_lo), (w_lo, x_hi))):
                    mm = pe.matmul(feat_ps[:, c, :], w[:, 0, e, lhs], xs[:, g, :], start=(i == 0), stop=(i == 2))
                mm.then_inc(hid_mm, 1)

            def down(g, u):
                e, c = (u // C) % E, u % C
                n = g * UE + u
                if u % 2:
                    pe.wait_ge(ghi_dve, g * (UE // 2) + (u // 2 + 1))
                else:
                    pe.wait_ge(ghi_act, g * (UE // 2) + (u // 2 + 1))
                pe.wait_ge(glo_done, n + 1)
                if c == 0 and not (isinstance(g, int) and g == 0 and e < 2):
                    pe.wait_ge(gated_done, g * E + u // C - 1)
                if isinstance(n, int) and n == C:
                    pe.wait_ge(x1_done, B)
                lhs = slice(c * P, (c + 1) * P)
                for i, (w, xs) in enumerate(((w_hi, gel_hi), (w_hi, gel_lo), (w_lo, gel_hi))):
                    mm = pe.matmul((x_ps, mix_ps)[e % 2][:], w[:, 1, e, lhs], xs[:, c, :],
                                   start=(c == 0 and i == 0), stop=(c == C - 1 and i == 2))
                mm.then_inc(down_mm, 1)

            def back_of(part, start, stop):
                for t in range(TG):
                    mm = pe.matmul(kv_ps[:, t * P:(t + 1) * P], part[:, t * P:(t + 1) * P], ident_s[:],
                                   start=(start and t == 0), stop=(stop and t == TG - 1))
                return mm

            def body(g, units, tail):
                if units:
                    pe.wait_ge(xhi_done, g + 1)
                    pe.wait_ge(xlo_done, g + 1)
                for u in range(UE if units else 8):
                    if not units and u == 0:
                        pe.wait_ge(res_done, g - 1)
                        pe.wait_ge(acc_done, g * 7 - 2)
                        back_of(acc, True, False)
                    if units:
                        if not (isinstance(g, int) and g == 0 and u < 4):
                            pe.wait_ge(gelu_done, g * UE + (u - 3))
                        up(g, u)
                    if (units and u >= LAG) or (tail and u < LAG):
                        down(g, u - LAG)
                    if is_first(g) and u == 1:
                        atok_of(B - 1)
                    if is_first(g) and u == 2:
                        xn2T_of(B - 2)
                    if is_first(g) and u == 3:
                        pe.wait_ge(xn2T_sb, B - 1)
                        attnT_of(B - 1)
                    if is_first(g) and u == 4:
                        y_of(B - 1)
                    if is_first(g) and u == 11:
                        xn2T_of(B - 1)
                    if is_first(g) and u == 15:
                        logits_of(1)
                    if is_first(g) and u in GATES_AT:
                        q = GATES_AT[u]
                        pe.wait_ge(gates_done, (1, 2, 2, 3)[q])
                        if q == 1:
                            pe.wait_ge(shifted, 2)
                        if q >= 2:
                            pe.wait_ge(gateT_sb, q)
                        for t in range(TG):
                            mm = pe.transpose(gate_bank(q)[0:E, t * P:(t + 1) * P], gate[:, 4 * q + t, :], ident_s[:])
                        mm.then_inc(gateT_ps, 1)
                    if tail and u == 7:
                        if units:
                            if not (isinstance(g, int) and g == 1):
                                pe.wait_ge(res_done, g - 1)
                            pe.wait_ge(acc_done, g * 7)
                            for t in range(TG):
                                mm = pe.transpose(kv_ps[:, t * P:(t + 1) * P], acc[:, t * P:(t + 1) * P], ident_s[:])
                        else:
                            pe.wait_ge(gated_done, g * E - 1)
                            back_of(gated[:, 0, :], False, False)
                            pe.wait_ge(gated_done, g * E)
                            mm = back_of(gated[:, 1, :], False, True)
                        mm.then_inc(back_ps, 1)

            groups(pe, body)


_OUT = (B, N, D)


def kernel(L0_attn_x, L0_attn_W_qkv, L0_attn_proj, L0_attn_W_out, L0_attn_b_out, L0_ffn_w_router,
           L0_ffn_w1, L0_ffn_b1, L0_ffn_w2, L0_ffn_b2):
    import numpy as np
    import concourse.bacc as bacc
    from concourse.bass_utils import run_bass_kernel_spmd

    proj = np.asarray(L0_attn_proj)
    proj3 = np.zeros((3, HG, HD, G, HG, F), proj.dtype)
    for j in range(HG):
        proj3[:, j, :, :, j, :] = proj.reshape(G, HG, HD, F)[:, j].transpose(1, 0, 2)
    w1 = np.asarray(L0_ffn_w1)
    w2 = np.asarray(L0_ffn_w2).reshape(E, C, P, D).transpose(0, 2, 1, 3).reshape(E, P, C * D)
    arrays = {
        "x": np.asarray(L0_attn_x).reshape(T * P, D),
        "wqkvT": np.asarray(L0_attn_W_qkv).T,
        "proj3": np.concatenate([proj3.reshape(96, H * F), np.ones((1, H * F), proj.dtype)]),
        "woT": np.asarray(L0_attn_W_out).T.reshape(2, 2, HG, HD, D).transpose(0, 2, 1, 3, 4).reshape(D, D),
        "bout": np.tile(np.asarray(L0_attn_b_out).reshape(1, D), (P, 1)),
        "wr": np.asarray(L0_ffn_w_router),
        "wcat": np.stack([w1, w2], axis=2),
        "b1": np.asarray(L0_ffn_b1).reshape(E, C, P).transpose(2, 0, 1),
        "b2": np.asarray(L0_ffn_b2).T,
        "ident": np.eye(P, dtype=np.float32),
        "expert_no": np.tile(np.arange(E, dtype=np.float32), (P, 1)),
    }
    arrays = {k: np.ascontiguousarray(v) for k, v in arrays.items()}
    nc = bacc.Bacc("TRN2", target_bir_lowering=False, num_devices=1)
    args = [nc.dram_tensor(k, v.shape, mybir.dt.from_np(v.dtype), kind="ExternalInput").ap() for k, v in arrays.items()]
    out = nc.dram_tensor("out", (T * P, D), F32, kind="ExternalOutput").ap()
    gates_dram = nc.dram_tensor("gates_dram", (E, T * P), F32, kind="Internal").ap()
    build(nc, *args, gates_dram, out)
    r = run_bass_kernel_spmd(nc, [arrays], core_ids=[0])
    return r.results[0]["out"].reshape(B, N, D)
```
